# Optimizing a Trainium2 kernel written in Bass

```python
import numpy as np
import jax
import jax.numpy as jnp

def _softmax(x, axis=-1):
    return jax.nn.softmax(x, axis=axis)

def _gelu(x):
    return jax.nn.gelu(x, approximate=True)

def _silu(x):
    return jax.nn.silu(x)

def _sigmoid(x):
    return jax.nn.sigmoid(x)

def _layernorm(x, axis=-1, eps=1e-05):
    m = jnp.mean(x, axis=axis, keepdims=True)
    v = jnp.var(x, axis=axis, keepdims=True)
    return (x - m) / jnp.sqrt(v + eps)

def _scatter_add(tgt, idx, src, axis=0):
    return tgt.at[idx].add(src)

def _segment_sum(src, seg, n):
    return jax.ops.segment_sum(src, seg, n)
kernel_name = 'mk_seq_postln_d1_jaxref_r8_d150b4'

def setup_inputs(seed: int=0):
    np.random.seed(seed)
    _w = jnp.asarray

    def _L0_attn_setup():
        import jax, jax.numpy as jnp
        import numpy as np
        DIM = 128
        DIM_HEAD = 16
        HEADS = 8
        EPS = 1e-05

        def rms_norm(x, gamma):
            n = jnp.sqrt(jnp.sum(x * x, axis=-1, keepdims=True))
            return gamma * (x / jnp.maximum(n, 1e-12)) * x.shape[-1] ** 0.5

        def second_taylor_expansion(x):
            d = x.shape[-1]
            x0 = jnp.ones(x.shape[:-1] + (1,), dtype=x.dtype)
            x2 = jnp.einsum('...i,...j->...ij', x, x) * 0.5 ** 0.5
            x2 = x2.reshape(x.shape[:-1] + (d * d,))
            return jnp.concatenate([x0, x, x2], axis=-1)
        key = jax.random.key(seed)
        ks = jax.random.split(key, 4)
        b, n = (4, 1024)
        dim_inner = DIM_HEAD * HEADS
        x = jax.random.normal(ks[0], (b, n, DIM), dtype=jnp.float32)
        gamma = jnp.ones((DIM,), dtype=jnp.float32)
        w_q = jax.random.normal(ks[1], (DIM, dim_inner), dtype=jnp.float32) * DIM ** (-0.5)
        w_kv = jax.random.normal(ks[2], (DIM, dim_inner * 2), dtype=jnp.float32) * DIM ** (-0.5)
        w_out = jax.random.normal(ks[3], (dim_inner, DIM), dtype=jnp.float32) * dim_inner ** (-0.5)
        return {'x': x, 'gamma': gamma, 'w_q': w_q, 'w_kv': w_kv, 'w_out': w_out}
    _L0_attn_in = _L0_attn_setup()

    def _L0_ffn_setup():
        import jax, jax.numpy as jnp
        import numpy as np
        D_IN, D_HID = (128, 512)

        def _ternary(key, shape):
            return jax.random.randint(key, shape, -1, 2).astype(jnp.float32)

        def _tlin(x, w, s):
            return jnp.einsum('bsi,oi->bso', x, w) * s
        key = jax.random.key(seed)
        ks = jax.random.split(key, 12)
        inv = lambda fan: 1.0 / np.sqrt(fan).astype(np.float32)
        return {'x': jax.random.normal(ks[0], (4, 256, D_IN), dtype=jnp.float32), 'w1_w': _ternary(ks[1], (D_HID, D_IN)), 'w1_s': jax.random.uniform(ks[2], (D_HID,), dtype=jnp.float32) * inv(D_IN), 'w2_w': _ternary(ks[3], (D_HID, D_IN)), 'w2_s': jax.random.uniform(ks[4], (D_HID,), dtype=jnp.float32) * inv(D_IN), 'h1_w': _ternary(ks[5], (D_HID, D_HID)), 'h1_s': jax.random.uniform(ks[6], (D_HID,), dtype=jnp.float32) * inv(D_HID), 'h2_w': _ternary(ks[7], (D_HID, D_HID)), 'h2_s': jax.random.uniform(ks[8], (D_HID,), dtype=jnp.float32) * inv(D_HID), 'w3_w': _ternary(ks[9], (D_IN, D_HID)), 'w3_s': jax.random.uniform(ks[10], (D_IN,), dtype=jnp.float32) * inv(D_HID)}
    _L0_ffn_in = _L0_ffn_setup()
    _d = {'L0_attn_x': _L0_attn_in['x'], 'L0_attn_gamma': _L0_attn_in['gamma'], 'L0_attn_w_q': _L0_attn_in['w_q'], 'L0_attn_w_kv': _L0_attn_in['w_kv'], 'L0_attn_w_out': _L0_attn_in['w_out'], 'L0_ffn_w1_w': _L0_ffn_in['w1_w'], 'L0_ffn_w1_s': _L0_ffn_in['w1_s'], 'L0_ffn_w2_w': _L0_ffn_in['w2_w'], 'L0_ffn_w2_s': _L0_ffn_in['w2_s'], 'L0_ffn_h1_w': _L0_ffn_in['h1_w'], 'L0_ffn_h1_s': _L0_ffn_in['h1_s'], 'L0_ffn_h2_w': _L0_ffn_in['h2_w'], 'L0_ffn_h2_s': _L0_ffn_in['h2_s'], 'L0_ffn_w3_w': _L0_ffn_in['w3_w'], 'L0_ffn_w3_s': _L0_ffn_in['w3_s']}
    _x0 = _d['L0_attn_x']
    _d['L0_attn_x'] = jax.random.normal(jax.random.fold_in(jax.random.key(seed), 1), (16, 512, 128), dtype=_x0.dtype)
    del _x0
    return _d

def reference(L0_attn_x, L0_attn_gamma, L0_attn_w_q, L0_attn_w_kv, L0_attn_w_out, L0_ffn_w1_w, L0_ffn_w1_s, L0_ffn_w2_w, L0_ffn_w2_s, L0_ffn_h1_w, L0_ffn_h1_s, L0_ffn_h2_w, L0_ffn_h2_s, L0_ffn_w3_w, L0_ffn_w3_s):

    def _L0_attn_ref(x, gamma, w_q, w_kv, w_out):
        import jax, jax.numpy as jnp
        import numpy as np
        DIM = 128
        DIM_HEAD = 16
        HEADS = 8
        EPS = 1e-05

        def rms_norm(x, gamma):
            n = jnp.sqrt(jnp.sum(x * x, axis=-1, keepdims=True))
            return gamma * (x / jnp.maximum(n, 1e-12)) * x.shape[-1] ** 0.5

        def second_taylor_expansion(x):
            d = x.shape[-1]
            x0 = jnp.ones(x.shape[:-1] + (1,), dtype=x.dtype)
            x2 = jnp.einsum('...i,...j->...ij', x, x) * 0.5 ** 0.5
            x2 = x2.reshape(x.shape[:-1] + (d * d,))
            return jnp.concatenate([x0, x, x2], axis=-1)
        b, n, _ = x.shape
        h, dh = (HEADS, DIM_HEAD)
        normed = rms_norm(x, gamma)
        q = (normed @ w_q).reshape(b, n, h, dh).transpose(0, 2, 1, 3)
        kv = (normed @ w_kv).reshape(b, n, 2, h, dh).transpose(2, 0, 3, 1, 4)
        k, v = (kv[0], kv[1])
        q = q * dh ** (-0.5)
        q = second_taylor_expansion(q)
        k = second_taylor_expansion(k)
        kv_state = jnp.einsum('bhnd,bhne->bhde', k, v)
        k_sum = jnp.sum(k, axis=2)
        den = jnp.einsum('bhnd,bhd->bhn', q, k_sum)
        qk_inv = 1.0 / jnp.maximum(den, EPS)
        out = jnp.einsum('bhnd,bhde->bhne', q, kv_state) * qk_inv[..., None]
        out = out.transpose(0, 2, 1, 3).reshape(b, n, h * dh)
        return out @ w_out

    def _L0_ffn_ref(x, w1_w, w1_s, w2_w, w2_s, h1_w, h1_s, h2_w, h2_s, w3_w, w3_s):
        import jax, jax.numpy as jnp
        import numpy as np
        D_IN, D_HID = (128, 512)

        def _ternary(key, shape):
            return jax.random.randint(key, shape, -1, 2).astype(jnp.float32)

        def _tlin(x, w, s):
            return jnp.einsum('bsi,oi->bso', x, w) * s
        h = jax.nn.silu(_tlin(x, w1_w, w1_s)) * _tlin(x, w2_w, w2_s)
        h = jax.nn.gelu(_tlin(h, h1_w, h1_s), approximate=False)
        h = jax.nn.gelu(_tlin(h, h2_w, h2_s), approximate=False)
        return _tlin(h, w3_w, w3_s)
    x = L0_attn_x
    x = _layernorm(x + _L0_attn_ref(x, L0_attn_gamma, L0_attn_w_q, L0_attn_w_kv, L0_attn_w_out), axis=-1)
    x = _layernorm(x + _L0_ffn_ref(x, L0_ffn_w1_w, L0_ffn_w1_s, L0_ffn_w2_w, L0_ffn_w2_s, L0_ffn_h1_w, L0_ffn_h1_s, L0_ffn_h2_w, L0_ffn_h2_s, L0_ffn_w3_w, L0_ffn_w3_s), axis=-1)
    return x

_drawn_inputs = setup_inputs


def setup_inputs(seed=0):
    import zlib

    import numpy as np

    out = dict(_drawn_inputs(seed))
    spreads = {'L0_attn_gamma': (1.0, 0.2)}
    factors = {'L0_ffn_w1_w': 8.0,
     'L0_ffn_w1_s': 8.0,
     'L0_ffn_w2_w': 8.0,
     'L0_ffn_w2_s': 8.0,
     'L0_ffn_h1_w': 8.0,
     'L0_ffn_h1_s': 8.0,
     'L0_ffn_h2_w': 8.0,
     'L0_ffn_h2_s': 8.0,
     'L0_ffn_w3_w': 8.0,
     'L0_ffn_w3_s': 8.0}
    for name, (base, spread) in spreads.items():
        noise = np.random.default_rng([zlib.crc32(name.encode()), seed]).standard_normal(out[name].shape)
        drawn = base * np.exp(spread * noise) if base else spread * noise
        out[name] = jnp.asarray(drawn.astype(out[name].dtype))
    for name, factor in factors.items():
        out[name] = (out[name] * factor).astype(out[name].dtype)
    return out
```

```python
from contextlib import ExitStack

import concourse.bass as bass
from concourse import mybir

F32 = mybir.dt.float32
F32R = mybir.dt.float32r
ALU = mybir.AluOpType
ACT = mybir.ActivationFunctionType
AX = mybir.AxisListType

P = 128
H, DH = 8, 16
EXT = 24
MAIN, REST = 128, 32
FEAT = MAIN + REST
LIN, PROD8, ONE = 0, 16, 24
LN_EPS, DEN_EPS, NORM_EPS = 1e-5, 1e-5, 1e-12

U_XT, U_QKV, U_STATE, U_STATE_T, U_PHI_T, U_OUT = 0, 1, 5, 6, 7, 17
A_USES = 18
PHI_ORDER = [0, 2, 4, 6, 1, 3, 5, 7, 8, 9]

G_XT, G_L1, G_L2, G_L3, G_W3, G_YT = 0, 1, 9, 13, 17, 18
F_BANK = [3] + [0, 1, 2, 3] * 2 + [0, 1, 2, 3] + [0, 1, 2, 3] + [0, 1]
F_USES = len(F_BANK)
F_PER_BANK = [F_BANK.count(b) for b in range(4)]


def is_positive(count):
    return not isinstance(count, int) or count > 0


def ring_before(i, u):
    return (A_USES // 2) * i + u // 2


def f_before(f, g):
    return F_PER_BANK[F_BANK[g]] * f + F_BANK[:g].count(F_BANK[g])


def build(nc, x, gamma, w_q, w_kv, w_out, w1t, s1, w2t, s2, h1t, hs1, h2t, hs2, w3t, s3, eye, out):
    B, N, D = x.shape
    HID = w1t.shape[1]
    NT = N // P
    KT = HID // P
    assert D == P and H * DH == P and NT == 4 and KT == 4 and B % 2 == 0

    x_d = x.rearrange("b (p j) d -> b p j d", j=NT)
    out_d = out.rearrange("b (p j) d -> b p j d", j=NT)

    with ExitStack() as ctx:
        def sb(name, shape, dt=F32):
            return ctx.enter_context(nc.sbuf_tensor(name, shape, dt))

        def sem(name):
            return ctx.enter_context(nc.semaphore(name))

        ring = ctx.enter_context(nc.psum_tensor("ring", [P, 2, 512], F32))
        acc = ctx.enter_context(nc.psum_tensor("acc", [P, 2, 512], F32))
        fps = ctx.enter_context(nc.psum_tensor("fps", [P, 4, 512], F32))

        w_qkv_raw = sb("w_qkv_raw", [P, 3, P])
        w_qkv = sb("w_qkv", [P, 3, P])
        w_o = sb("w_o", [P, P])
        ident = sb("ident", [P, P])
        col = sb("col", [P, 24])
        gam_c, s3_c = col[:, 0:1], col[:, 1:2]
        s1_c, s2_c, hs1_c, hs2_c = (col[:, 4 * n:4 * n + 4] for n in range(1, 5))
        half_c = col[:, 2:3]
        neg_half = sb("neg_half", [P, NT])
        WN = 2 * HID + 2 * KT * HID + KT * D
        w_hi = sb("w_hi", [P, WN], F32R)
        w_lo = sb("w_lo", [P, WN], F32R)
        o1, o2, oh1, oh2, o3 = 0, HID, 2 * HID, 2 * HID + KT * HID, 2 * HID + 2 * KT * HID

        x_b = [sb(f"x_b{p}", [P, NT, D]) for p in range(2)]
        sq = sb("sq", [P, NT, D])
        ss = sb("ss", [P, NT])
        ssc = sb("ssc", [P, NT])
        rn = sb("rn", [P, NT])
        xn = sb("xn", [P, NT, D])
        xnT = sb("xnT", [P, N])
        kq = sb("kq", [P, NT, 2 * H, EXT])
        v_one = sb("v_one", [P, NT, H, 2 * DH])
        phi_k = sb("phi_k", [P, NT, H, FEAT])
        phi_q = sb("phi_q", [P, NT * H * FEAT])
        phi_qm = phi_q[:, 0:NT * H * MAIN].rearrange("p (j h f) -> p j h f", j=NT, h=H)
        phi_qr = phi_q[:, NT * H * MAIN:].rearrange("p (j h f) -> p j h f", j=NT, h=H)
        st = sb("st", [P, 2, FEAT])
        restT = sb("restT", [P, 2, 2, DH])
        mask = sb("mask", [P, 4, DH])
        w_main = sb("w_main", [P, 2, 4, 4, DH])
        w_rest = sb("w_rest", [P, 2, 2, 4, DH])
        phiT = sb("phiT", [P, 10, N])
        raw_a = phi_k[:, :, :, :].rearrange("p j h f -> p (j h f)")
        raw_b = phiT[:, :, :].rearrange("p f n -> p (f n)")
        den = sb("den", [P, N])
        rden = sb("rden", [P, N])
        att = sb("att", [P, N])
        x1p = sb("x1p", [P, NT, D])
        stats = sb("stats", [P, NT, 6])
        mv = sb("mv", [P, NT, 2])
        veps = sb("veps", [P, NT])
        rstd = sb("rstd", [P, NT])
        x1 = [sb(f"x1_{p}", [P, NT, D]) for p in range(2)]

        x1T = [sb(f"x1T_{n}", [P, N], F32R) for n in ("hi", "lo")]
        gate = sb("gate", [P, 2, N])
        h32 = sb("h32", [P, 4, N])
        hid = [[sb(f"hid{s}_{n}", [P, KT, N], F32R) for n in ("hi", "lo")] for s in range(2)]
        yT = sb("yT", [P, N])
        z = sb("z", [P, NT, D])
        zstats = sb("zstats", [P, NT, 6])
        zmv = sb("zmv", [P, NT, 2])
        zveps = sb("zveps", [P, NT])
        zrstd = sb("zrstd", [P, NT])
        o_b = [sb(f"o_b{p}", [P, NT, D]) for p in range(2)]

        consts_loaded, qkv_w_loaded, ffn_w_loaded = sem("consts_loaded"), sem("qkv_w_loaded"), sem("ffn_w_loaded")
        x_loaded = [sem(f"x_loaded{p}") for p in range(2)]
        stored = [sem(f"stored{p}") for p in range(2)]
        zeroed = sem("zeroed")
        consts_set = sem("consts_set")
        qkv_w_ready, w_hi_ready, w_ready = sem("qkv_w_ready"), sem("w_hi_ready"), sem("w_ready")
        sq_ready, ss_ready, ssc_ready, rn_ready, xn_ready = (
            sem(n) for n in ("sq_ready", "ss_ready", "ssc_ready", "rn_ready", "xn_ready"))
        ring_full = sem("ring_full")
        ring_free = [sem(f"ring_free{b}") for b in range(2)]
        phi_main_ready, phi_rest_ready = sem("phi_main_ready"), sem("phi_rest_ready")
        restT_ready, w_rest_ready = sem("restT_ready"), sem("w_rest_ready")
        acc_full = sem("acc_full")
        den_ready, rden_ready, att_ready = sem("den_ready"), sem("rden_ready"), sem("att_ready")
        mv_ready, veps_ready, rstd_ready, x1_ready = (
            sem(n) for n in ( "mv_ready", "veps_ready", "rstd_ready", "x1_ready"))
        f_full = sem("f_full")
        f_free = [sem(f"f_free{b}") for b in range(4)]
        x1hi_ready = sem("x1hi_ready")
        hi_ready, split_ready = sem("hi_ready"), sem("split_ready")
        zmv_ready, zveps_ready, zrstd_ready, out_ready = (
            sem(n) for n in ( "zmv_ready", "zveps_ready", "zrstd_ready", "out_ready"))

        block = ctx.enter_context(nc.Block())

        def steps(eng, step):
            step(0, 0, True, False)
            step(1, 1, True, True)
            step(2, 0, True, True)
            with eng.Fori(0, B // 2 - 2) as r:
                for half in range(2):
                    step(2 * r + 3 + half, (1 + half) % 2, True, True)
            step(B - 1, 1, True, True)
            step(B, 0, False, True)

        @block.sync
        def _(sp):
            sp.dma_start(x_b[0][:, :, :], x_d[0]).then_inc(x_loaded[0], 16)
            sp.dma_start(ident[:, :], eye).then_inc(consts_loaded, 16)
            sp.dma_start(gam_c, gamma).then_inc(consts_loaded, 16)
            sp.dma_start(s3_c, s3).then_inc(consts_loaded, 16)
            for c, s in ((s1_c, s1), (s2_c, s2), (hs1_c, hs1), (hs2_c, hs2)):
                sp.dma_start(c, s).then_inc(consts_loaded, 16)
            sp.dma_start(w_qkv_raw[:, 0, :], w_kv[:, 0:P]).then_inc(qkv_w_loaded, 16)
            sp.dma_start(w_qkv_raw[:, 1, :], w_q).then_inc(qkv_w_loaded, 16)
            sp.dma_start(w_qkv_raw[:, 2, :], w_kv[:, P:2 * P]).then_inc(qkv_w_loaded, 16)
            sp.dma_start(w_o[:, :], w_out).then_inc(qkv_w_loaded, 16)
            for o, w, k in ((o1, w1t, 1), (o2, w2t, 1), (oh1, h1t, KT), (oh2, h2t, KT), (o3, w3t, KT)):
                n = w.shape[1]
                raw = raw_b[:, 0:k * n] if o == o3 else raw_a[:, o:o + k * n]
                sp.dma_start(raw.rearrange("p (k n) -> p k n", k=k),
                             w.rearrange("(k p) n -> p k n", p=P)).then_inc(ffn_w_loaded, 16)

            def step(t, par, attn, ffn):
                if attn and not (isinstance(t, int) and t == B - 1):
                    if is_positive(t):
                        sp.wait_ge(ring_free[U_OUT % 2], ring_before(t - 1, U_OUT) + 1)
                    sp.dma_start(x_b[1 - par][:, :, :],
                                 x_d[bass.ds(t + 1, 1)].rearrange("b p j d -> (b p) j d")
                                 ).then_inc(x_loaded[1 - par], 16)
                if ffn:
                    sp.wait_ge(out_ready, t)
                    sp.dma_start(out_d[bass.ds(t - 1, 1)].rearrange("b p j d -> (b p) j d"),
                                 o_b[1 - par][:, :, :]).then_inc(stored[1 - par], 16)

            steps(sp, step)
            for p in range(2):
                sp.wait_ge(stored[p], 16 * (B // 2))

        @block.tensor
        def _(pe):
            def ring_wait(i, u):
                if is_positive(ring_before(i, u)):
                    pe.wait_ge(ring_free[u % 2], ring_before(i, u))

            def ring_read(i, u):
                pe.wait_ge(ring_free[u % 2], ring_before(i, u) + 1)

            def f_wait(f, g):
                if is_positive(f_before(f, g)):
                    pe.wait_ge(f_free[F_BANK[g]], f_before(f, g))

            def transpose_x(i):
                pe.wait_ge(xn_ready, i + 1)
                ring_wait(i, U_XT)
                for j in range(NT):
                    mm = nc.tensor.transpose(ring[:, 0, j * P:(j + 1) * P], xn[:, j, :], ident[:, :])
                mm.then_inc(ring_full, 1)

            def project_qkv(i):
                ring_read(i, U_XT)
                for j in range(NT):
                    ring_wait(i, U_QKV + j)
                    nc.tensor.matmul(ring[:, (U_QKV + j) % 2, 0:3 * P], xnT[:, j * P:(j + 1) * P],
                                     w_qkv[:, :, :].rearrange("p a n -> p (a n)"),
                                     start=True, stop=True).then_inc(ring_full, 1)

            def state(i):
                ring_wait(i, U_STATE)
                for g in range(2):
                    for j in range(NT):
                        if g == 0:
                            pe.wait_ge(phi_main_ready, NT * i + j + 1)
                            pe.wait_ge(phi_rest_ready, NT * i + j + 1)
                        for hh in range(4):
                            mm = nc.tensor.matmul(ring[32 * hh:32 * hh + 32, U_STATE % 2, g * FEAT:(g + 1) * FEAT],
                                                  v_one[:, j, 4 * g + hh, :], phi_k[:, j, 4 * g + hh, :],
                                                  start=(j == 0), stop=(j == NT - 1))
                mm.then_inc(ring_full, 1)

            def transpose_state(i):
                ring_wait(i, U_STATE_T)
                ring_read(i, U_STATE)
                for g in range(2):
                    mm = nc.tensor.transpose(ring[:, U_STATE_T % 2, g * P:(g + 1) * P], st[:, g, 0:MAIN], ident[:, :])
                mm.then_inc(ring_full, 1)

            def transpose_phi(i, n):
                u, f = U_PHI_T + n, PHI_ORDER[n]
                ring_wait(i, u)
                for j in range(NT):
                    src = phi_qm[:, j, f, :] if f < H else \
                        phi_qr[:, j, 4 * (f - H):4 * (f - H) + 4, :].rearrange("p h r -> p (h r)")
                    mm = nc.tensor.transpose(ring[:, u % 2, j * P:(j + 1) * P], src, ident[:, :])
                mm.then_inc(ring_full, 1)

            def apply_main(i, b):
                for n in (4 * b + 2, 4 * b + 3):
                    ring_read(i, U_PHI_T + n)
                for nd in range(2):
                    for c in range(4):
                        nc.tensor.matmul(acc[32 * c:32 * c + 32, nd, :],
                                         w_main[:, nd, c, 2 * b:2 * b + 2, :].rearrange("p a e -> p (a e)"),
                                         phiT[:, 2 * c + b, :], start=(b == 0), stop=False)

            def apply_rest(i):
                for n in (8, 9):
                    ring_read(i, U_PHI_T + n)
                pe.wait_ge(w_rest_ready, 2 * i + 2)
                for nd in range(2):
                    for c in range(4):
                        g, cc = c // 2, c % 2
                        mm = nc.tensor.matmul(acc[32 * c:32 * c + 32, nd, :],
                                              w_rest[:, g, nd, 2 * cc:2 * cc + 2, :].rearrange("p a e -> p (a e)"),
                                              phiT[:, H + g, :], start=False, stop=True)
                mm.then_inc(acc_full, 1)

            def project_out(i):
                pe.wait_ge(att_ready, i + 1)
                ring_wait(i, U_OUT)
                for j in range(NT):
                    mm = nc.tensor.matmul(ring[:, U_OUT % 2, j * P:(j + 1) * P], att[:, j * P:(j + 1) * P], w_o[:, :],
                                          start=True, stop=True)
                mm.then_inc(ring_full, 1)

            def transpose_x1(f, par):
                pe.wait_ge(x1_ready, f + 1)
                f_wait(f, G_XT)
                for j in range(NT):
                    mm = nc.tensor.transpose(fps[:, F_BANK[G_XT], j * P:(j + 1) * P], x1[par][:, j, :], ident[:, :])
                mm.then_inc(f_full, 1)

            def product(bank, o, hi, lo, start, stop):
                nc.tensor.matmul(fps[:, bank, :], w_hi[:, o:o + P], hi, start=start, stop=False)
                nc.tensor.matmul(fps[:, bank, :], w_hi[:, o:o + P], lo, start=False, stop=False)
                return nc.tensor.matmul(fps[:, bank, :], w_lo[:, o:o + P], hi, start=False, stop=stop)

            def layer1(f, m):
                for n, o in ((0, o1), (1, o2)):
                    g = G_L1 + 2 * m + n
                    f_wait(f, g)
                    if g == G_L1:
                        pe.wait_ge(f_free[F_BANK[G_XT]], f_before(f, G_XT) + 1)
                    product(F_BANK[g], o + m * P, x1T[0][:, :], x1T[1][:, :], True, True).then_inc(f_full, 1)

            def hidden(f, g, o, wide, src, before, m, ks=range(4)):
                if 0 in ks:
                    f_wait(f, g)
                for k in ks:
                    if m == 0:
                        pe.wait_ge(split_ready, 3 * KT * f + before + k + 1)
                    mm = product(F_BANK[g], o + k * wide + m * P, hid[src][0][:, k, :], hid[src][1][:, k, :],
                                 k == 0, k == KT - 1)
                if KT - 1 in ks:
                    mm.then_inc(f_full, 1)

            def layer2(f, m, ks=range(4)):
                hidden(f, G_L2 + m, oh1, HID, 0, 0, m, ks)

            def layer3(f, m, ks=range(4)):
                hidden(f, G_L3 + m, oh2, HID, 1, KT, m, ks)

            def layer4(f):
                hidden(f, G_W3, o3, D, 0, 2 * KT, 0)

            def transpose_y(f):
                pe.wait_ge(f_free[F_BANK[G_W3]], f_before(f, G_W3) + 1)
                f_wait(f, G_YT)
                for j in range(NT):
                    mm = nc.tensor.transpose(fps[:, F_BANK[G_YT], j * P:(j + 1) * P], yT[:, j * P:(j + 1) * P],
                                             ident[:, :])
                mm.then_inc(f_full, 1)

            def step(t, par, attn, ffn):
                i, f = t, t - 1
                if attn:
                    transpose_x(i)
                    project_qkv(i)
                if ffn:
                    transpose_x1(f, 1 - par)
                    for m in range(KT):
                        layer1(f, m)
                    for m in range(KT):
                        layer2(f, m)
                if attn:
                    state(i)
                if ffn:
                    layer3(f, 0)
                if attn:
                    transpose_state(i)
                    transpose_phi(i, 0)
                    transpose_phi(i, 1)
                if ffn:
                    layer3(f, 1, (0, 1))
                if attn:
                    transpose_phi(i, 2)
                    transpose_phi(i, 3)
                if ffn:
                    layer3(f, 1, (2, 3))
                if attn:
                    transpose_phi(i, 4)
                    transpose_phi(i, 5)
                    apply_main(i, 0)
                    transpose_phi(i, 6)
                    transpose_phi(i, 7)
                if ffn:
                    layer3(f, 2, (0, 1))
                if attn:
                    transpose_phi(i, 8)
                    transpose_phi(i, 9)
                    apply_main(i, 1)
                if ffn:
                    layer3(f, 2, (2, 3))
                if attn:
                    apply_rest(i)
                if ffn:
                    layer3(f, 3)
                if attn:
                    project_out(i)
                if ffn:
                    layer4(f)
                    transpose_y(f)

            pe.wait_ge(consts_loaded, 16 * 7)
            pe.wait_ge(qkv_w_ready, 3)
            pe.wait_ge(qkv_w_loaded, 16 * 4)
            pe.wait_ge(w_ready, 2)
            steps(pe, step)

        @block.scalar
        def _(act):
            def square(i, par):
                act.wait_ge(x_loaded[par], 8 * (i + 2 - par))
                if is_positive(i):
                    act.wait_ge(ss_ready, i)
                nc.scalar.activation(sq[:, :, :], x_b[par][:, :, :], ACT.Square).then_inc(sq_ready, 1)

            def ring_copy(i, u, out, in_, scale=1.0, last=True):
                act.wait_ge(ring_full, A_USES * i + u + 1)
                op = nc.scalar.activation(out, in_, ACT.Copy, scale=scale)
                if last:
                    op.then_inc(ring_free[u % 2], 1)

            def copy_qkv(i, j):
                u = U_QKV + j
                bank = ring[:, u % 2, :]
                groups = bank[:, 0:2 * P].rearrange("p (g e) -> p g e", e=DH)
                if is_positive(i) and j == 0:
                    act.wait_ge(phi_main_ready, NT * i)
                    act.wait_ge(phi_rest_ready, NT * i)
                ring_copy(i, u, kq[:, j, :, 0:DH], groups, last=False)
                ring_copy(i, u, kq[:, j, :, DH:EXT], groups[:, :, 0:EXT - DH], last=False)
                ring_copy(i, u, v_one[:, j, :, 0:DH], bank[:, 2 * P:3 * P].rearrange("p (h e) -> p h e", e=DH))

            def copy_state_T(i):
                src = ring[:, U_STATE_T % 2, 0:2 * P].rearrange("p (c b n e) -> p c b n e", c=4, b=2, n=2)
                for nd in range(2):
                    ring_copy(i, U_STATE_T, w_main[:, nd, :, 0:4:3, :], src[:, :, :, nd, :], half_c, last=(nd == 1))

            def copy_phi_T(i, n):
                u = U_PHI_T + n
                ring_copy(i, u, phiT[:, PHI_ORDER[n], :], ring[:, u % 2, :])

            def x1_hi(f):
                act.wait_ge(f_full, F_USES * f + G_XT + 1)
                nc.scalar.activation(x1T[0][:, :], fps[:, F_BANK[G_XT], :], ACT.Copy).then_inc(x1hi_ready, 1)

            def silu(f, m):
                g = G_L1 + 2 * m
                act.wait_ge(f_full, F_USES * f + g + 1)
                if m >= 2:
                    act.wait_ge(f_free[F_BANK[g - 3]], f_before(f, g - 3) + 1)
                nc.scalar.activation(gate[:, m % 2, :], fps[:, F_BANK[g], :], ACT.Silu, scale=s1_c[:, m:m + 1])\
                    .then_inc(f_free[F_BANK[g]], 1)

            def gelu(f, layer, m):
                g = (G_L2, G_L3)[layer] + m
                n = KT * (layer + 1) + m
                act.wait_ge(f_full, F_USES * f + g + 1)
                act.wait_ge(split_ready, 3 * KT * f + n - 3)
                nc.scalar.activation(h32[:, n % 4, :], fps[:, F_BANK[g], :], ACT.Gelu,
                                     scale=(hs1_c, hs2_c)[layer][:, m:m + 1]).then_inc(f_free[F_BANK[g]], 1)

            def copy_y(f):
                act.wait_ge(f_full, F_USES * f + G_W3 + 1)
                nc.scalar.activation(yT[:, :], fps[:, F_BANK[G_W3], :], ACT.Copy, scale=s3_c)\
                    .then_inc(f_free[F_BANK[G_W3]], 1)

            def step(t, par, attn, ffn):
                i, f = t, t - 1
                if attn:
                    ring_copy(i, U_XT, xnT[:, :], ring[:, 0, :])
                    for j in range(NT):
                        copy_qkv(i, j)
                if ffn:
                    x1_hi(f)
                    for m in range(KT):
                        silu(f, m)
                if attn and not (isinstance(t, int) and t == B - 1):
                    square(i + 1, 1 - par)
                if ffn:
                    for m in range(KT):
                        gelu(f, 0, m)
                if attn:
                    ring_copy(i, U_STATE, st[:, :, :].rearrange("p g f -> p (g f)"),
                              ring[:, U_STATE % 2, 0:2 * FEAT])
                if ffn:
                    gelu(f, 1, 0)
                if attn:
                    copy_state_T(i)
                    for n in range(4):
                        copy_phi_T(i, n)
                if ffn:
                    gelu(f, 1, 1)
                if attn:
                    for n in range(4, 10):
                        copy_phi_T(i, n)
                if ffn:
                    gelu(f, 1, 2)
                    gelu(f, 1, 3)
                    copy_y(f)

            act.wait_ge(consts_loaded, 16 * 7)
            act.wait_ge(consts_set, 2)
            square(0, 0)
            steps(act, step)

        @block.vector
        def _(dve):
            def sum_squares(i):
                dve.wait_ge(sq_ready, i + 1)
                nc.vector.tensor_reduce(ss[:, :], sq[:, :, :], AX.X, ALU.add).then_inc(ss_ready, 1)
                dve.wait_ge(ss_ready, i + 1)
                if is_positive(i):
                    dve.wait_ge(rn_ready, i)
                nc.vector.tensor_scalar(ssc[:, :], ss[:, :], NORM_EPS ** 2, 1.0 / D, ALU.max, ALU.mult)\
                    .then_inc(ssc_ready, 1)

            def phi_main(i, j):
                dve.wait_ge(ring_free[(U_QKV + j) % 2], ring_before(i, U_QKV + j) + 1)
                if is_positive(i):
                    dve.wait_ge(ring_full, A_USES * (i - 1) + U_PHI_T + 10)
                for h0, out in ((0, phi_k[:, j, :, 0:MAIN]), (H, phi_qm[:, j, :, :])):
                    base = kq[:, j, h0:h0 + H, 0:DH]
                    part, (hs, hn), (es, en) = base.ap[0], base.ap[1], base.ap[2]
                    fixed = bass.AP(base.tensor, base.offset, [part, [hs, hn], [0, 8], [es, en]])
                    moved = bass.AP(base.tensor, base.offset, [part, [hs, hn], [1, 8], [es, en]])
                    op = nc.vector.tensor_tensor(out.rearrange("p h (s e) -> p h s e", e=DH), fixed, moved, ALU.mult)
                op.then_inc(phi_main_ready, 1)

            def rest_T(i):
                dve.wait_ge(ring_free[U_STATE % 2], ring_before(i, U_STATE) + 1)
                if is_positive(i):
                    dve.wait_ge(w_rest_ready, 2 * i)
                for g in range(2):
                    op = nc.vector.transpose(restT[:, g, :, :].rearrange("p n e -> p (n e)"), st[:, g, MAIN:FEAT])
                op.then_inc(restT_ready, 1)

            def normalise(i):
                dve.wait_ge(acc_full, i + 1)
                nc.vector.tensor_scalar(den[:, :], acc[:, 1, :], DEN_EPS, None, ALU.max).then_inc(den_ready, 1)
                dve.wait_ge(den_ready, i + 1)
                nc.vector.reciprocal(rden[:, :], den[:, :]).then_inc(rden_ready, 1)
                dve.wait_ge(rden_ready, i + 1)
                nc.vector.tensor_tensor(att[:, :], acc[:, 0, :], rden[:, :], ALU.mult).then_inc(att_ready, 1)

            def norm_scale(n, par, sm, mv2, rs, s_mv, s_rs, dst, ready):
                dve.wait_ge(s_mv, n + 1)
                dve.wait_ge(s_rs, n + 1)
                for j in range(NT):
                    op = nc.vector.tensor_scalar(dst[:, j, :], sm[:, j, :], mv2[:, j, 0:1], rs[:, j:j + 1],
                                                 ALU.subtract, ALU.mult)
                op.then_inc(ready, 1)

            def sum_x1(i, par):
                dve.wait_ge(ring_full, A_USES * i + U_OUT + 1)
                nc.vector.tensor_tensor(x1p[:, :, :].rearrange("p j d -> p (j d)"),
                                        x_b[par][:, :, :].rearrange("p j d -> p (j d)"), ring[:, U_OUT % 2, :],
                                        ALU.add).then_inc(ring_free[U_OUT % 2], 1)
                dve.wait_ge(ring_free[U_OUT % 2], ring_before(i, U_OUT) + 1)
                for j in range(NT):
                    nc.vector.bn_stats(stats[:, j, :], x1p[:, j, :])
                dve.drain()
                for j in range(NT):
                    op = nc.vector.bn_aggr(mv[:, j, :], stats[:, j, :])
                op.then_inc(mv_ready, 1)
                dve.wait_ge(mv_ready, i + 1)
                nc.vector.tensor_scalar(veps[:, :], mv[:, :, 1], LN_EPS, None, ALU.add).then_inc(veps_ready, 1)

            def sum_z(f, par):
                dve.wait_ge(f_full, F_USES * f + G_YT + 1)
                nc.vector.tensor_tensor(z[:, :, :].rearrange("p j d -> p (j d)"),
                                        x1[par][:, :, :].rearrange("p j d -> p (j d)"), fps[:, F_BANK[G_YT], :],
                                        ALU.add).then_inc(f_free[F_BANK[G_YT]], 1)
                dve.wait_ge(f_free[F_BANK[G_YT]], f_before(f, G_YT) + 1)
                for j in range(NT):
                    nc.vector.bn_stats(zstats[:, j, :], z[:, j, :])
                dve.drain()
                for j in range(NT):
                    op = nc.vector.bn_aggr(zmv[:, j, :], zstats[:, j, :])
                op.then_inc(zmv_ready, 1)
                dve.wait_ge(zmv_ready, f + 1)
                nc.vector.tensor_scalar(zveps[:, :], zmv[:, :, 1], LN_EPS, None, ALU.add).then_inc(zveps_ready, 1)

            def x1_lo(f):
                dve.wait_ge(x1hi_ready, f + 1)
                nc.vector.tensor_tensor(x1T[1][:, :], fps[:, F_BANK[G_XT], :], x1T[0][:, :].bitcast(F32),
                                        ALU.subtract).then_inc(f_free[F_BANK[G_XT]], 1)

            def split(f, n, dst):
                hi, lo = hid[dst][0][:, n % KT, :], hid[dst][1][:, n % KT, :]
                nc.vector.tensor_copy(hi, h32[:, n % 4, :]).then_inc(hi_ready, 1)
                dve.wait_ge(hi_ready, 3 * KT * f + n + 1)
                nc.vector.tensor_tensor(lo, h32[:, n % 4, :], hi.bitcast(F32), ALU.subtract).then_inc(split_ready, 1)

            def gated_tile(f, m):
                g = G_L1 + 2 * m + 1
                dve.wait_ge(f_full, F_USES * f + g + 1)
                dve.wait_ge(f_free[F_BANK[g - 1]], f_before(f, g - 1) + 1)
                nc.vector.scalar_tensor_tensor(out=h32[:, m, :], in0=fps[:, F_BANK[g], :], scalar=s2_c[:, m:m + 1],
                                               in1=gate[:, m % 2, :], op0=ALU.mult, op1=ALU.mult)\
                    .then_inc(f_free[F_BANK[g]], 1)
                dve.wait_ge(f_free[F_BANK[g]], f_before(f, g) + 1)
                split(f, m, 0)

            def gelu_tile(f, layer, m):
                g = (G_L2, G_L3)[layer] + m
                dve.wait_ge(f_free[F_BANK[g]], f_before(f, g) + 1)
                split(f, KT * (layer + 1) + m, 1 - layer)

            def step(t, par, attn, ffn):
                i, f = t, t - 1
                if ffn:
                    x1_lo(f)
                for m in range(KT):
                    if ffn:
                        gated_tile(f, m)
                    if attn:
                        phi_main(i, m)
                if attn and not (isinstance(t, int) and t == B - 1):
                    sum_squares(i + 1)
                if ffn:
                    for m in range(KT):
                        gelu_tile(f, 0, m)
                if attn:
                    rest_T(i)
                if ffn:
                    for m in range(3):
                        gelu_tile(f, 1, m)
                if attn:
                    normalise(i)
                if ffn:
                    gelu_tile(f, 1, 3)
                if attn:
                    sum_x1(i, par)
                if ffn:
                    sum_z(f, 1 - par)
                if attn:
                    norm_scale(i, par, x1p, mv, rstd, mv_ready, rstd_ready, x1[par], x1_ready)
                if ffn:
                    if is_positive(t - 2):
                        dve.wait_ge(stored[1 - par], 8 * (t - 2 + par))
                    norm_scale(f, par, z, zmv, zrstd, zmv_ready, zrstd_ready, o_b[1 - par], out_ready)

            nc.vector.memset(half_c, 1.0).then_inc(zeroed, 1)
            nc.vector.memset(mask[:, :, :], 0.0).then_inc(zeroed, 1)
            dve.wait_ge(zeroed, 2)
            nc.vector.memset(half_c[0:DH, :], 0.5)
            for hh in range(4):
                op = nc.vector.memset(mask[32 * hh:32 * hh + 32, hh, :], 1.0)
            op.then_inc(consts_set, 1)
            dve.wait_ge(consts_loaded, 16 * 7)
            dve.wait_ge(qkv_w_loaded, 16 * 4)
            nc.vector.tensor_scalar(w_qkv[:, 0, :], w_qkv_raw[:, 0, :], gam_c, None, ALU.mult).then_inc(qkv_w_ready, 1)
            nc.vector.tensor_scalar(w_qkv[:, 1, :], w_qkv_raw[:, 1, :], gam_c, DH ** -0.5, ALU.mult, ALU.mult)\
                .then_inc(qkv_w_ready, 1)
            nc.vector.tensor_scalar(w_qkv[:, 2, :], w_qkv_raw[:, 2, :], gam_c, None, ALU.mult).then_inc(qkv_w_ready, 1)
            sum_squares(0)
            dve.wait_ge(ffn_w_loaded, 16 * 5)
            for n, (raw, a, b) in enumerate(((raw_b, o3, WN), (raw_a, 0, o3))):
                nc.vector.tensor_copy(w_hi[:, a:b], raw[:, 0:b - a]).then_inc(w_hi_ready, 1)
                dve.wait_ge(w_hi_ready, n + 1)
                nc.vector.tensor_tensor(w_lo[:, a:b], raw[:, 0:b - a], w_hi[:, a:b].bitcast(F32), ALU.subtract)\
                    .then_inc(w_ready, 1)
            steps(dve, step)

        @block.gpsimd
        def _(pool):
            def normed_x(i, par):
                pool.wait_ge(ssc_ready, i + 1)
                nc.gpsimd.tensor_tensor(rn[:, :], ssc[:, :], neg_half[:, :], ALU.pow).then_inc(rn_ready, 1)
                pool.wait_ge(rn_ready, i + 1)
                if is_positive(i):
                    pool.wait_ge(ring_full, A_USES * (i - 1) + U_XT + 1)
                nc.gpsimd.tensor_tensor(xn[:, :, :], x_b[par][:, :, :],
                                        rn[:, :].unsqueeze(2).to_broadcast([P, NT, D]), ALU.mult)\
                    .then_inc(xn_ready, 1)

            def phi_rest(i, j):
                pool.wait_ge(ring_free[(U_QKV + j) % 2], ring_before(i, U_QKV + j) + 1)
                if is_positive(i):
                    pool.wait_ge(ring_full, A_USES * (i - 1) + U_PHI_T + 10)
                for h0, rest in ((0, phi_k[:, j, :, MAIN:FEAT]), (H, phi_qr[:, j, :, :])):
                    src = kq[:, j, h0:h0 + H, :]
                    nc.gpsimd.tensor_tensor(rest[:, :, PROD8:PROD8 + 8], src[:, :, 0:8], src[:, :, 8:16], ALU.mult)
                    op = nc.gpsimd.tensor_copy(rest[:, :, LIN:LIN + DH], src[:, :, 0:DH])
                op.then_inc(phi_rest_ready, 1)

            def weights_rest(i):
                pool.wait_ge(restT_ready, i + 1)
                if is_positive(i):
                    pool.wait_ge(acc_full, i)
                for g in range(2):
                    src = restT[:, g, :, :].unsqueeze(2).to_broadcast([P, 2, 4, DH])
                    msk = mask[:, :, :].unsqueeze(1).to_broadcast([P, 2, 4, DH])
                    nc.gpsimd.tensor_tensor(w_rest[:, g, :, :, :], src, msk, ALU.mult).then_inc(w_rest_ready, 1)

            def inv_std(n, var_ready, var, rs, rs_ready):
                pool.wait_ge(var_ready, n + 1)
                nc.gpsimd.tensor_tensor(rs[:, :], var[:, :], neg_half[:, :], ALU.pow).then_inc(rs_ready, 1)

            def step(t, par, attn, ffn):
                i, f = t, t - 1
                if attn:
                    for j in range(NT):
                        phi_rest(i, j)
                    if not (isinstance(t, int) and t == B - 1):
                        normed_x(i + 1, 1 - par)
                    weights_rest(i)
                    inv_std(i, veps_ready, veps, rstd, rstd_ready)
                if ffn:
                    inv_std(f, zveps_ready, zveps, zrstd, zrstd_ready)

            nc.gpsimd.memset(neg_half[:, :], -0.5)
            nc.gpsimd.memset(w_main[:, :, :, :, :], 0.0)
            nc.gpsimd.memset(v_one[:, :, :, :], 1.0).then_inc(consts_set, 1)
            pool.wait_ge(consts_set, 2)
            normed_x(0, 0)
            pool.wait_ge(w_ready, 2)
            for j in range(NT):
                for rest in (phi_k[:, j, :, MAIN:FEAT], phi_qr[:, j, :, :]):
                    nc.gpsimd.memset(rest[:, :, ONE:ONE + 1], 1.0)
                    nc.gpsimd.memset(rest[:, :, ONE + 1:REST], 0.0)
            steps(pool, step)


_F = ["L0_ffn_w1", "L0_ffn_w2", "L0_ffn_h1", "L0_ffn_h2", "L0_ffn_w3"]


def kernel(**inputs):
    import numpy as _np
    import concourse.bacc as _bacc
    from concourse import mybir as _mybir
    from concourse.bass_utils import run_bass_kernel_spmd as _run

    a = {k: _np.ascontiguousarray(v) for k, v in inputs.items()}
    data = {
        "x": a["L0_attn_x"], "gamma": a["L0_attn_gamma"].reshape(-1, 1),
        "w_q": a["L0_attn_w_q"], "w_kv": a["L0_attn_w_kv"], "w_out": a["L0_attn_w_out"],
    }
    for name in _F:
        data[name + "_w"] = _np.ascontiguousarray(a[name + "_w"].T)
        data[name + "_s"] = _np.ascontiguousarray(a[name + "_s"].reshape(-1, 128).T)
    data["eye"] = _np.eye(128, dtype=_np.float32)

    nc = _bacc.Bacc("TRN2", target_bir_lowering=False, num_devices=1)
    arrays, args = {}, []
    for name, arr in data.items():
        arrays[f"in_{name}"] = arr
        args.append(nc.dram_tensor(f"in_{name}", arr.shape, _mybir.dt.from_np(arr.dtype), kind="ExternalInput").ap())
    args.append(nc.dram_tensor("out_0", data["x"].shape, _mybir.dt.float32, kind="ExternalOutput").ap())
    build(nc, *args)
    r = _run(nc, [arrays], core_ids=[0])
    return r.results[0]["out_0"]
```

```python
from contextlib import ExitStack

import concourse.bass as bass
from concourse import mybir

F32 = mybir.dt.float32
F32R = mybir.dt.float32r
ALU = mybir.AluOpType
ACT = mybir.ActivationFunctionType
AX = mybir.AxisListType

P = 128
H, DH = 8, 16
MAIN, REST = 128, 32
FEAT = MAIN + REST
DUP, ONE, PROD8 = 16, 23, 24
LN_EPS, DEN_EPS, NORM_EPS = 1e-5, 1e-5, 1e-12

FRONT, MIDDLE, FFN, TAIL = range(4)

RING = [(what, stage, n % 2) for n, (what, stage) in enumerate((
    ("state", MIDDLE), ("phi8", MIDDLE), ("phi9", MIDDLE), ("stateT", MIDDLE), ("xT", FRONT),
    ("phi0", MIDDLE), ("phi2", MIDDLE), ("qkv0", FRONT), ("phi4", MIDDLE), ("phi6", MIDDLE), ("qkv1", FRONT),
    ("phi1", MIDDLE), ("phi3", MIDDLE), ("qkv2", FRONT), ("phi5", MIDDLE), ("phi7", MIDDLE),
    ("out", MIDDLE), ("qkv3", FRONT)))]
FPS = [(what, stage, n % 4) for n, (what, stage) in enumerate((
    ("a0", FFN), ("b0", FFN), ("a1", FFN), ("b1", FFN), ("a2", FFN), ("b2", FFN), ("a3", FFN), ("b3", FFN),
    ("yT", TAIL), ("two0", FFN), ("two1", FFN), ("two2", FFN), ("two3", FFN),
    ("three0", FFN), ("three1", FFN), ("three2", FFN), ("three3", FFN), ("x1T", MIDDLE), ("y", FFN)))]


def is_positive(count):
    return not isinstance(count, int) or count > 0


def bank_of(table, what):
    return next(b for w, _, b in table if w == what)


def writes_before(table, batches, t, what, bank=None):
    if not isinstance(t, int):
        full = max(stage for _, stage, _ in table)
        per_step = sum(bank in (None, b) for _, _, b in table)
        return per_step * (t - full) + writes_before(table, batches, full, what, bank)
    at = [w for w, _, _ in table].index(what)
    return sum(bank in (None, b) and (step < t or n < at) and 0 <= step - stage < batches
               for step in range(t + 1) for n, (_, stage, b) in enumerate(table))


def build(nc, x, gamma, w_q, w_kv, w_out, w1t, s1, w2t, s2, h1t, hs1, h2t, hs2, w3t, s3, consts, out):
    B, N, D = x.shape
    HID = w1t.shape[1]
    NT = N // P
    KT = HID // P
    assert D == P and H * DH == P and NT == 4 and KT == 4 and B % 2 == 0

    x_d = x.rearrange("b (p j) d -> b p j d", j=NT)
    out_d = out.rearrange("b (p j) d -> b p j d", j=NT)

    with ExitStack() as ctx:
        def sb(name, shape, dt=F32):
            return ctx.enter_context(nc.sbuf_tensor(name, shape, dt))

        def sem(name):
            return ctx.enter_context(nc.semaphore(name))

        ring = ctx.enter_context(nc.psum_tensor("ring", [P, 2, 512], F32))
        acc = ctx.enter_context(nc.psum_tensor("acc", [P, 2, 512], F32))
        fps = ctx.enter_context(nc.psum_tensor("fps", [P, 4, 512], F32))

        w_qkv_raw = sb("w_qkv_raw", [P, 3, P])
        w_qkv = sb("w_qkv", [P, 3, P])
        w_o = sb("w_o", [P, P])
        const = sb("const", [P, P + 4 * DH + NT + 1])
        ident = const[:, 0:P]
        mask = const[:, P:P + 4 * DH].rearrange("p (h e) -> p h e", h=4)
        neg_half = const[:, P + 4 * DH:P + 4 * DH + NT]
        half_c = const[:, P + 4 * DH + NT:]
        col = sb("col", [P, 24])
        gam_c, s3_c = col[:, 0:1], col[:, 1:2]
        s1_c, s2_c, hs1_c, hs2_c = (col[:, 4 * n:4 * n + 4] for n in range(1, 5))
        WN = 2 * HID + 2 * KT * HID + KT * D
        w_hi = sb("w_hi", [P, WN], F32R)
        w_lo = sb("w_lo", [P, WN], F32R)
        o1, o2, oh1, oh2, o3 = 0, HID, 2 * HID, 2 * HID + KT * HID, 2 * HID + 2 * KT * HID

        x_b = [sb(f"x_b{p}", [P, NT, D]) for p in range(2)]
        sq = sb("sq", [P, NT, D])
        ss = sb("ss", [P, NT])
        ssc = sb("ssc", [P, NT])
        rn = sb("rn", [P, NT])
        xn = sb("xn", [P, NT, D])
        xnT = sb("xnT", [P, N])
        v_one = sb("v_one", [P, NT, H, 2 * DH])
        phi_k = sb("phi_k", [P, NT, H, FEAT])
        phi_q = sb("phi_q", [P, NT * H * FEAT])
        phi_qm = phi_q[:, 0:NT * H * MAIN].rearrange("p (j h f) -> p j h f", j=NT, h=H)
        phi_qr = phi_q[:, NT * H * MAIN:].rearrange("p (j h f) -> p j h f", j=NT, h=H)
        st = sb("st", [P, 2, FEAT])
        restT = sb("restT", [P, 2, 2, DH])
        w_main = sb("w_main", [P, 2, 4, 4, DH])
        w_rest = sb("w_rest", [P, 2, 2, 4, DH])
        phiT = sb("phiT", [P, 10, N])
        raw_a = phi_k[:, :, :, :].rearrange("p j h f -> p (j h f)")
        raw_b = phiT[:, :, :].rearrange("p f n -> p (f n)")
        den = sb("den", [P, N])
        rden = sb("rden", [P, N])
        att = sb("att", [P, N])
        x1p = sb("x1p", [P, NT, D])
        stats = sb("stats", [P, NT, 6])
        mv = sb("mv", [P, NT, 2])
        veps = sb("veps", [P, NT])
        rstd = sb("rstd", [P, NT])
        x1 = [sb(f"x1_{p}", [P, NT, D]) for p in range(2)]

        x1T = [sb(f"x1T_{n}", [P, N], F32R) for n in ("hi", "lo")]
        gate = sb("gate", [P, 2, N])
        h32 = sb("h32", [P, 4, N])
        hid = [[sb(f"hid{s}_{n}", [P, KT, N], F32R) for n in ("hi", "lo")] for s in range(2)]
        yT = sb("yT", [P, N])
        z = sb("z", [P, NT, D])
        zstats = sb("zstats", [P, NT, 6])
        zmv = sb("zmv", [P, NT, 2])
        zveps = sb("zveps", [P, NT])
        zrstd = sb("zrstd", [P, NT])
        o_b = sb("o_b", [P, NT, D])
        lo_max = sb("lo_max", [P, 1])
        lo_max1 = sb("lo_max1", [1, 1])

        consts_loaded, qkv_w_loaded, ffn_w_loaded = sem("consts_loaded"), sem("qkv_w_loaded"), sem("ffn_w_loaded")
        x_loaded = [sem(f"x_loaded{p}") for p in range(2)]
        stored = sem("stored")
        consts_set = sem("consts_set")
        lo_max_ready, lo_max_T, lo_max1_ready = sem("lo_max_ready"), sem("lo_max_T"), sem("lo_max1_ready")
        qkv_w_ready, w_hi_ready, w_ready = sem("qkv_w_ready"), sem("w_hi_ready"), sem("w_ready")
        sq_ready, ss_ready, ssc_ready, rn_ready, xn_ready = (
            sem(n) for n in ("sq_ready", "ss_ready", "ssc_ready", "rn_ready", "xn_ready"))
        ring_full = sem("ring_full")
        ring_free = [sem(f"ring_free{b}") for b in range(2)]
        phi_k_ready, phi_q_ready, prod8_ready = sem("phi_k_ready"), sem("phi_q_ready"), sem("prod8_ready")
        restT_ready, w_rest_ready = sem("restT_ready"), sem("w_rest_ready")
        acc_full = sem("acc_full")
        den_ready, rden_ready, att_ready = sem("den_ready"), sem("rden_ready"), sem("att_ready")
        mv_ready, veps_ready, rstd_ready, x1_ready = (
            sem(n) for n in ( "mv_ready", "veps_ready", "rstd_ready", "x1_ready"))
        f_full = sem("f_full")
        f_free = [sem(f"f_free{b}") for b in range(4)]
        x1hi_ready = sem("x1hi_ready")
        hi_ready, split_ready = sem("hi_ready"), sem("split_ready")
        zmv_ready, zveps_ready, zrstd_ready, out_ready = (
            sem(n) for n in ( "zmv_ready", "zveps_ready", "zrstd_ready", "out_ready"))

        block = ctx.enter_context(nc.Block())

        def steps(eng, step):
            def peeled(t):
                step(t, t % 2, *(0 <= t - stage < B for stage in range(4)))

            for t in range(3):
                peeled(t)
            with eng.Fori(0, B // 2 - 2) as r:
                for half in range(2):
                    step(2 * r + 3 + half, (1 + half) % 2, True, True, True, True)
            for t in range(B - 1, B + 3):
                peeled(t)

        def written(table, t, what):
            return writes_before(table, B, t, what) + 1

        def read(table, t, what):
            return writes_before(table, B, t, what, bank_of(table, what)) + 1

        def is_last(t):
            return isinstance(t, int) and t == B - 1

        @block.sync
        def _(sp):
            sp.dma_start(x_b[0][:, :, :], x_d[0]).then_inc(x_loaded[0], 16)
            sp.dma_start(const[:, :], consts).then_inc(consts_loaded, 16)
            sp.dma_start(gam_c, gamma).then_inc(consts_loaded, 16)
            sp.dma_start(s3_c, s3).then_inc(consts_loaded, 16)
            for c, s in ((s1_c, s1), (s2_c, s2), (hs1_c, hs1), (hs2_c, hs2)):
                sp.dma_start(c, s).then_inc(consts_loaded, 16)
            sp.dma_start(w_qkv_raw[:, 0, :], w_kv[:, 0:P]).then_inc(qkv_w_loaded, 16)
            sp.dma_start(w_qkv_raw[:, 1, :], w_q).then_inc(qkv_w_loaded, 16)
            sp.dma_start(w_qkv_raw[:, 2, :], w_kv[:, P:2 * P]).then_inc(qkv_w_loaded, 16)
            sp.dma_start(w_o[:, :], w_out).then_inc(qkv_w_loaded, 16)
            for o, w, k in ((o1, w1t, 1), (o2, w2t, 1), (oh1, h1t, KT), (oh2, h2t, KT), (o3, w3t, KT)):
                n = w.shape[1]
                raw = raw_b[:, 0:k * n] if o == o3 else raw_a[:, o:o + k * n]
                sp.dma_start(raw.rearrange("p (k n) -> p k n", k=k),
                             w.rearrange("(k p) n -> p k n", p=P)).then_inc(ffn_w_loaded, 16)

            def step(t, par, front, middle, ffn, tail):
                if front and not is_last(t):
                    if middle:
                        sp.wait_ge(ring_free[bank_of(RING, "out")], read(RING, t, "out"))
                    sp.dma_start(x_b[1 - par][:, :, :],
                                 x_d[bass.ds(t + 1, 1)].rearrange("b p j d -> (b p) j d")
                                 ).then_inc(x_loaded[1 - par], 16)
                if tail:
                    sp.wait_ge(out_ready, t - 2)
                    sp.dma_start(out_d[bass.ds(t - 3, 1)].rearrange("b p j d -> (b p) j d"), o_b[:, :, :])\
                        .then_inc(stored, 16)

            steps(sp, step)
            sp.wait_ge(stored, 16 * B)

        @block.tensor
        def _(pe):
            def bank_wait(table, free, t, what):
                before = read(table, t, what) - 1
                if is_positive(before):
                    pe.wait_ge(free[bank_of(table, what)], before)

            def transpose_x(t):
                pe.wait_ge(xn_ready, t + 1)
                bank_wait(RING, ring_free, t, "xT")
                for j in range(NT):
                    mm = nc.tensor.transpose(ring[:, bank_of(RING, "xT"), j * P:(j + 1) * P], xn[:, j, :], ident)
                mm.then_inc(ring_full, 1)

            def project_qkv(t, j):
                if j == 0:
                    pe.wait_ge(ring_free[bank_of(RING, "xT")], read(RING, t, "xT"))
                bank_wait(RING, ring_free, t, f"qkv{j}")
                nc.tensor.matmul(ring[:, bank_of(RING, f"qkv{j}"), 0:3 * P], xnT[:, j * P:(j + 1) * P],
                                 w_qkv[:, :, :].rearrange("p a n -> p (a n)"),
                                 start=True, stop=True).then_inc(ring_full, 1)

            def state(t):
                bank = bank_of(RING, "state")
                bank_wait(RING, ring_free, t, "state")
                for g in range(2):
                    for j in range(NT):
                        if g == 0:
                            pe.wait_ge(phi_k_ready, NT * (t - 1) + j + 1)
                            pe.wait_ge(prod8_ready, NT * (t - 1) + j + 1)
                        for hh in range(4):
                            mm = nc.tensor.matmul(ring[32 * hh:32 * hh + 32, bank, g * FEAT:(g + 1) * FEAT],
                                                  v_one[:, j, 4 * g + hh, :], phi_k[:, j, 4 * g + hh, :],
                                                  start=(j == 0), stop=(j == NT - 1))
                mm.then_inc(ring_full, 1)

            def transpose_state(t):
                pe.wait_ge(ring_free[bank_of(RING, "state")], read(RING, t, "state"))
                bank_wait(RING, ring_free, t, "stateT")
                for g in range(2):
                    mm = nc.tensor.transpose(ring[:, bank_of(RING, "stateT"), g * P:(g + 1) * P],
                                             st[:, g, 0:MAIN], ident)
                mm.then_inc(ring_full, 1)

            def transpose_phi(t, f):
                what = f"phi{f}"
                bank_wait(RING, ring_free, t, what)
                if f == 8:
                    pe.wait_ge(prod8_ready, NT * t)
                for j in range(NT):
                    if f == 0:
                        pe.wait_ge(phi_q_ready, NT * (t - 1) + j + 1)
                    src = phi_qm[:, j, f, :] if f < H else \
                        phi_qr[:, j, 4 * (f - H):4 * (f - H) + 4, :].rearrange("p h r -> p (h r)")
                    mm = nc.tensor.transpose(ring[:, bank_of(RING, what), j * P:(j + 1) * P], src, ident)
                mm.then_inc(ring_full, 1)

            def apply_main(t, b):
                for f in (b + 4, b + 6):
                    pe.wait_ge(ring_free[bank_of(RING, f"phi{f}")], read(RING, t, f"phi{f}"))
                for nd in range(2):
                    for c in range(4):
                        nc.tensor.matmul(acc[32 * c:32 * c + 32, nd, :],
                                         w_main[:, nd, c, 2 * b:2 * b + 2, :].rearrange("p a e -> p (a e)"),
                                         phiT[:, 2 * c + b, :], start=(b == 0), stop=False)

            def apply_rest(t):
                pe.wait_ge(w_rest_ready, 2 * t)
                for nd in (1, 0):
                    for c in range(4):
                        g, cc = c // 2, c % 2
                        mm = nc.tensor.matmul(acc[32 * c:32 * c + 32, nd, :],
                                              w_rest[:, g, nd, 2 * cc:2 * cc + 2, :].rearrange("p a e -> p (a e)"),
                                              phiT[:, H + g, :], start=False, stop=True)
                    mm.then_inc(acc_full, 1)

            def project_out(t):
                pe.wait_ge(att_ready, t)
                bank_wait(RING, ring_free, t, "out")
                for j in range(NT):
                    mm = nc.tensor.matmul(ring[:, bank_of(RING, "out"), j * P:(j + 1) * P],
                                          att[:, j * P:(j + 1) * P], w_o[:, :], start=True, stop=True)
                mm.then_inc(ring_full, 1)

            def transpose_x1(t, par):
                pe.wait_ge(x1_ready, t)
                bank_wait(FPS, f_free, t, "x1T")
                for j in range(NT):
                    mm = nc.tensor.transpose(fps[:, bank_of(FPS, "x1T"), j * P:(j + 1) * P], x1[par][:, j, :], ident)
                mm.then_inc(f_full, 1)

            def product(bank, o, hi, lo, start, stop, with_lo):
                nc.tensor.matmul(fps[:, bank, :], w_hi[:, o:o + P], hi, start=start, stop=False)
                mm = nc.tensor.matmul(fps[:, bank, :], w_hi[:, o:o + P], lo, start=False, stop=stop and not with_lo)
                if with_lo:
                    mm = nc.tensor.matmul(fps[:, bank, :], w_lo[:, o:o + P], hi, start=False, stop=stop)
                return mm

            def layer1(t, m, with_lo):
                for what, o in ((f"a{m}", o1), (f"b{m}", o2)):
                    bank_wait(FPS, f_free, t, what)
                    if what == "a0":
                        pe.wait_ge(f_free[bank_of(FPS, "x1T")], read(FPS, t - 1, "x1T"))
                    product(bank_of(FPS, what), o + m * P, x1T[0][:, :], x1T[1][:, :], True, True, with_lo)\
                        .then_inc(f_full, 1)

            def hidden(t, what, o, wide, src, before, m, with_lo):
                bank_wait(FPS, f_free, t, what)
                for k in range(KT):
                    if m == 0:
                        pe.wait_ge(split_ready, 3 * KT * (t - 2) + before + k + 1)
                    mm = product(bank_of(FPS, what), o + k * wide + m * P, hid[src][0][:, k, :],
                                 hid[src][1][:, k, :], k == 0, k == KT - 1, with_lo)
                mm.then_inc(f_full, 1)

            def layer2(t, m, with_lo):
                hidden(t, f"two{m}", oh1, HID, 0, 0, m, with_lo)

            def layer3(t, m, with_lo):
                hidden(t, f"three{m}", oh2, HID, 1, KT, m, with_lo)

            def layer4(t, with_lo):
                hidden(t, "y", o3, D, 0, 2 * KT, 0, with_lo)

            def transpose_y(t):
                pe.wait_ge(f_free[bank_of(FPS, "y")], read(FPS, t - 1, "y"))
                bank_wait(FPS, f_free, t, "yT")
                for j in range(NT):
                    mm = nc.tensor.transpose(fps[:, bank_of(FPS, "yT"), j * P:(j + 1) * P], yT[:, j * P:(j + 1) * P],
                                             ident)
                mm.then_inc(f_full, 1)

            def program(with_lo):
                def step(t, par, front, middle, ffn, tail):
                    if ffn:
                        layer1(t, 0, with_lo)
                    if middle:
                        state(t)
                    if ffn:
                        layer1(t, 1, with_lo)
                    if middle:
                        transpose_phi(t, 8)
                        transpose_phi(t, 9)
                    if ffn:
                        layer1(t, 2, with_lo)
                    if middle:
                        transpose_state(t)
                    if front:
                        transpose_x(t)
                    if ffn:
                        layer1(t, 3, with_lo)
                    if tail:
                        transpose_y(t)
                    if middle:
                        transpose_phi(t, 0)
                        transpose_phi(t, 2)
                    if front:
                        project_qkv(t, 0)
                    if middle:
                        transpose_phi(t, 4)
                        transpose_phi(t, 6)
                    if front:
                        project_qkv(t, 1)
                    if ffn:
                        layer2(t, 0, with_lo)
                    if middle:
                        apply_main(t, 0)
                        transpose_phi(t, 1)
                        transpose_phi(t, 3)
                    if front:
                        project_qkv(t, 2)
                    if middle:
                        transpose_phi(t, 5)
                        transpose_phi(t, 7)
                    if ffn:
                        layer2(t, 1, with_lo)
                    if middle:
                        apply_main(t, 1)
                        apply_rest(t)
                    if ffn:
                        layer2(t, 2, with_lo)
                        layer2(t, 3, with_lo)
                        layer3(t, 0, with_lo)
                    if middle:
                        project_out(t)
                    if ffn:
                        layer3(t, 1, with_lo)
                        layer3(t, 2, with_lo)
                        layer3(t, 3, with_lo)
                    if front:
                        project_qkv(t, 3)
                    if middle:
                        transpose_x1(t, 1 - par)
                    if ffn:
                        layer4(t, with_lo)

                steps(pe, step)

            pe.wait_ge(consts_loaded, 16 * 7)
            pe.wait_ge(qkv_w_ready, 3)
            pe.wait_ge(qkv_w_loaded, 16 * 4)
            pe.wait_ge(lo_max_ready, 1)
            nc.tensor.transpose(ring[0:1, 0, 0:P], lo_max[:, :], ident).then_inc(lo_max_T, 1)
            pe.wait_ge(lo_max1_ready, 1)
            lo_bits = pe.value_load(lo_max1[:, :].bitcast(mybir.dt.int32))
            with pe.If(lo_bits != 0):
                program(True)
            with pe.Else():
                program(False)

        @block.scalar
        def _(act):
            def square(t, par):
                act.wait_ge(x_loaded[par], 8 * (t + 2 - par))
                if is_positive(t):
                    act.wait_ge(ss_ready, t)
                nc.scalar.activation(sq[:, :, :], x_b[par][:, :, :], ACT.Square).then_inc(sq_ready, 1)

            def ring_copy(t, what, out, in_, scale=1.0, last=True):
                act.wait_ge(ring_full, written(RING, t, what))
                op = nc.scalar.activation(out, in_, ACT.Copy, scale=scale)
                if last:
                    op.then_inc(ring_free[bank_of(RING, what)], 1)

            def copy_qkv(t, j):
                bank = ring[:, bank_of(RING, f"qkv{j}"), :]
                k, q, v = (bank[:, a * P:(a + 1) * P].rearrange("p (h e) -> p h e", e=DH) for a in range(3))
                if is_positive(t) and j == 0:
                    act.wait_ge(phi_q_ready, NT * t)
                    act.wait_ge(prod8_ready, NT * t)
                for src, rest in ((k, phi_k[:, j, :, MAIN:FEAT]), (q, phi_qr[:, j, :, :])):
                    ring_copy(t, f"qkv{j}", rest[:, :, 0:DH], src, last=False)
                    ring_copy(t, f"qkv{j}", rest[:, :, DUP:ONE], src[:, :, 0:ONE - DUP], last=False)
                ring_copy(t, f"qkv{j}", v_one[:, j, :, 0:DH], v)

            def copy_state_T(t):
                src = ring[:, bank_of(RING, "stateT"), 0:2 * P].rearrange("p (c b n e) -> p c b n e", c=4, b=2, n=2)
                for nd in range(2):
                    ring_copy(t, "stateT", w_main[:, nd, :, 0:4:3, :], src[:, :, :, nd, :], half_c, last=(nd == 1))

            def copy_phi_T(t, *tiles):
                for f in tiles:
                    ring_copy(t, f"phi{f}", phiT[:, f, :], ring[:, bank_of(RING, f"phi{f}"), :])

            def x1_hi(t):
                act.wait_ge(f_full, written(FPS, t, "x1T"))
                nc.scalar.activation(x1T[0][:, :], fps[:, bank_of(FPS, "x1T"), :], ACT.Copy).then_inc(x1hi_ready, 1)

            def silu(t, m):
                act.wait_ge(f_full, written(FPS, t, f"a{m}"))
                if m >= 2:
                    act.wait_ge(f_free[bank_of(FPS, f"b{m - 2}")], read(FPS, t, f"b{m - 2}"))
                nc.scalar.activation(gate[:, m % 2, :], fps[:, bank_of(FPS, f"a{m}"), :], ACT.Silu,
                                     scale=s1_c[:, m:m + 1]).then_inc(f_free[bank_of(FPS, f"a{m}")], 1)

            def gelu(t, layer, m):
                what = f"{('two', 'three')[layer]}{m}"
                n = KT * (layer + 1) + m
                act.wait_ge(f_full, written(FPS, t, what))
                act.wait_ge(split_ready, 3 * KT * (t - 2) + n - 3)
                scale = (hs1_c, hs2_c)[layer][:, m:m + 1]
                bank = bank_of(FPS, what)
                nc.scalar.activation(h32[:, n % 4, :], fps[:, bank, :], ACT.Gelu, scale=scale)
                nc.scalar.activation(hid[1 - layer][0][:, m, :], fps[:, bank, :], ACT.Gelu, scale=scale)\
                    .then_inc(f_free[bank], 1)

            def copy_y(t):
                act.wait_ge(f_full, written(FPS, t, "y"))
                nc.scalar.activation(yT[:, :], fps[:, bank_of(FPS, "y"), :], ACT.Copy, scale=s3_c)\
                    .then_inc(f_free[bank_of(FPS, "y")], 1)

            def step(t, par, front, middle, ffn, tail):
                if ffn:
                    silu(t, 0)
                if front:
                    square(t, par)
                if middle:
                    ring_copy(t, "state", st[:, :, :].rearrange("p g f -> p (g f)"),
                              ring[:, bank_of(RING, "state"), 0:2 * FEAT])
                if ffn:
                    silu(t, 1)
                if middle:
                    copy_phi_T(t, 8, 9)
                if ffn:
                    silu(t, 2)
                if middle:
                    copy_state_T(t)
                if front:
                    ring_copy(t, "xT", xnT[:, :], ring[:, bank_of(RING, "xT"), :])
                if ffn:
                    silu(t, 3)
                if middle:
                    copy_phi_T(t, 0, 2)
                if front:
                    copy_qkv(t, 0)
                if middle:
                    copy_phi_T(t, 4, 6)
                if front:
                    copy_qkv(t, 1)
                if ffn:
                    gelu(t, 0, 0)
                if middle:
                    copy_phi_T(t, 1, 3)
                if front:
                    copy_qkv(t, 2)
                if middle:
                    copy_phi_T(t, 5, 7)
                if ffn:
                    gelu(t, 0, 1)
                    gelu(t, 0, 2)
                    gelu(t, 0, 3)
                    gelu(t, 1, 0)
                    gelu(t, 1, 1)
                    gelu(t, 1, 2)
                    gelu(t, 1, 3)
                if front:
                    copy_qkv(t, 3)
                if middle:
                    x1_hi(t)
                if ffn:
                    copy_y(t)

            act.wait_ge(consts_loaded, 16 * 7)
            act.wait_ge(consts_set, 1)
            steps(act, step)

        @block.vector
        def _(dve):
            def sum_squares(t):
                dve.wait_ge(sq_ready, t + 1)
                nc.vector.tensor_reduce(ss[:, :], sq[:, :, :], AX.X, ALU.add).then_inc(ss_ready, 1)
                dve.wait_ge(ss_ready, t + 1)
                if is_positive(t):
                    dve.wait_ge(rn_ready, t)
                nc.vector.tensor_scalar(ssc[:, :], ss[:, :], NORM_EPS ** 2, 1.0 / D, ALU.max, ALU.mult)\
                    .then_inc(ssc_ready, 1)

            def products(rest, out):
                base = rest[:, :, 0:DH]
                part, (hs, hn), (es, en) = base.ap[0], base.ap[1], base.ap[2]
                fixed = bass.AP(base.tensor, base.offset, [part, [hs, hn], [0, 8], [es, en]])
                moved = bass.AP(base.tensor, base.offset, [part, [hs, hn], [1, 8], [es, en]])
                return nc.vector.tensor_tensor(out.rearrange("p h (s e) -> p h s e", e=DH), fixed, moved, ALU.mult)

            def phi_k_main(t, j):
                dve.wait_ge(ring_free[bank_of(RING, f"qkv{j}")], read(RING, t, f"qkv{j}"))
                products(phi_k[:, j, :, MAIN:FEAT], phi_k[:, j, :, 0:MAIN]).then_inc(phi_k_ready, 1)

            def phi_q_main(t, j, middle):
                dve.wait_ge(ring_free[bank_of(RING, f"qkv{j}")], read(RING, t, f"qkv{j}"))
                if middle and j == 0:
                    dve.wait_ge(ring_full, written(RING, t, "phi7"))
                products(phi_qr[:, j, :, :], phi_qm[:, j, :, :]).then_inc(phi_q_ready, 1)

            def rest_T(t):
                dve.wait_ge(ring_free[bank_of(RING, "state")], read(RING, t, "state"))
                if is_positive(t - 1):
                    dve.wait_ge(w_rest_ready, 2 * t - 2)
                for g in range(2):
                    op = nc.vector.transpose(restT[:, g, :, :].rearrange("p n e -> p (n e)"), st[:, g, MAIN:FEAT])
                op.then_inc(restT_ready, 1)

            def normalise(t):
                dve.wait_ge(acc_full, 2 * t - 1)
                nc.vector.tensor_scalar(den[:, :], acc[:, 1, :], DEN_EPS, None, ALU.max).then_inc(den_ready, 1)
                dve.wait_ge(den_ready, t)
                nc.vector.reciprocal(rden[:, :], den[:, :]).then_inc(rden_ready, 1)
                dve.wait_ge(rden_ready, t)
                dve.wait_ge(acc_full, 2 * t)
                nc.vector.tensor_tensor(att[:, :], acc[:, 0, :], rden[:, :], ALU.mult).then_inc(att_ready, 1)

            def norm_scale(n, sm, mv2, rs, s_mv, s_rs, dst, ready):
                dve.wait_ge(s_mv, n + 1)
                dve.wait_ge(s_rs, n + 1)
                for j in range(NT):
                    op = nc.vector.tensor_scalar(dst[:, j, :], sm[:, j, :], mv2[:, j, 0:1], rs[:, j:j + 1],
                                                 ALU.subtract, ALU.mult)
                op.then_inc(ready, 1)

            def sum_x1(t, par):
                bank = bank_of(RING, "out")
                dve.wait_ge(ring_full, written(RING, t, "out"))
                nc.vector.tensor_tensor(x1p[:, :, :].rearrange("p j d -> p (j d)"),
                                        x_b[par][:, :, :].rearrange("p j d -> p (j d)"), ring[:, bank, :],
                                        ALU.add).then_inc(ring_free[bank], 1)
                dve.wait_ge(ring_free[bank], read(RING, t, "out"))
                for j in range(NT):
                    nc.vector.bn_stats(stats[:, j, :], x1p[:, j, :])
                dve.drain()
                for j in range(NT):
                    op = nc.vector.bn_aggr(mv[:, j, :], stats[:, j, :])
                op.then_inc(mv_ready, 1)
                dve.wait_ge(mv_ready, t)
                nc.vector.tensor_scalar(veps[:, :], mv[:, :, 1], LN_EPS, None, ALU.add).then_inc(veps_ready, 1)

            def sum_z(t, par):
                bank = bank_of(FPS, "yT")
                dve.wait_ge(f_full, written(FPS, t, "yT"))
                nc.vector.tensor_tensor(z[:, :, :].rearrange("p j d -> p (j d)"),
                                        x1[par][:, :, :].rearrange("p j d -> p (j d)"), fps[:, bank, :],
                                        ALU.add).then_inc(f_free[bank], 1)
                dve.wait_ge(f_free[bank], read(FPS, t, "yT"))
                for j in range(NT):
                    nc.vector.bn_stats(zstats[:, j, :], z[:, j, :])
                dve.drain()
                for j in range(NT):
                    op = nc.vector.bn_aggr(zmv[:, j, :], zstats[:, j, :])
                op.then_inc(zmv_ready, 1)
                dve.wait_ge(zmv_ready, t - 2)
                nc.vector.tensor_scalar(zveps[:, :], zmv[:, :, 1], LN_EPS, None, ALU.add).then_inc(zveps_ready, 1)

            def x1_lo(t):
                bank = bank_of(FPS, "x1T")
                dve.wait_ge(x1hi_ready, t)
                nc.vector.tensor_tensor(x1T[1][:, :], fps[:, bank, :], x1T[0][:, :].bitcast(F32),
                                        ALU.subtract).then_inc(f_free[bank], 1)

            def split(n, dst):
                hi, lo = hid[dst][0][:, n % KT, :], hid[dst][1][:, n % KT, :]
                nc.vector.tensor_tensor(lo, h32[:, n % 4, :], hi.bitcast(F32), ALU.subtract).then_inc(split_ready, 1)

            def gated_tile(t, m):
                a, b = f"a{m}", f"b{m}"
                dve.wait_ge(f_full, written(FPS, t, b))
                dve.wait_ge(f_free[bank_of(FPS, a)], read(FPS, t, a))
                nc.vector.scalar_tensor_tensor(out=h32[:, m, :], in0=fps[:, bank_of(FPS, b), :],
                                               scalar=s2_c[:, m:m + 1], in1=gate[:, m % 2, :], op0=ALU.mult,
                                               op1=ALU.mult).then_inc(f_free[bank_of(FPS, b)], 1)
                dve.wait_ge(f_free[bank_of(FPS, b)], read(FPS, t, b))
                nc.vector.tensor_copy(hid[0][0][:, m, :], h32[:, m, :]).then_inc(hi_ready, 1)
                dve.wait_ge(hi_ready, KT * (t - 2) + m + 1)
                split(m, 0)

            def gelu_tile(t, layer, m):
                what = f"{('two', 'three')[layer]}{m}"
                dve.wait_ge(f_free[bank_of(FPS, what)], read(FPS, t, what))
                split(KT * (layer + 1) + m, 1 - layer)

            def step(t, par, front, middle, ffn, tail):
                if ffn:
                    gated_tile(t, 0)
                if front:
                    sum_squares(t)
                if ffn:
                    gated_tile(t, 1)
                if middle:
                    rest_T(t)
                if ffn:
                    gated_tile(t, 2)
                    gated_tile(t, 3)
                if tail:
                    sum_z(t, 1 - par)
                if front:
                    phi_k_main(t, 0)
                if tail:
                    if is_positive(t - 3):
                        dve.wait_ge(stored, 16 * (t - 3))
                    norm_scale(t - 3, z, zmv, zrstd, zmv_ready, zrstd_ready, o_b, out_ready)
                if front:
                    phi_k_main(t, 1)
                if ffn:
                    gelu_tile(t, 0, 0)
                if front:
                    phi_k_main(t, 2)
                if ffn:
                    gelu_tile(t, 0, 1)
                if middle:
                    normalise(t)
                if ffn:
                    gelu_tile(t, 0, 2)
                    gelu_tile(t, 0, 3)
                if front:
                    phi_q_main(t, 0, middle)
                if ffn:
                    gelu_tile(t, 1, 0)
                if middle:
                    sum_x1(t, 1 - par)
                if front:
                    phi_q_main(t, 1, middle)
                if middle:
                    norm_scale(t - 1, x1p, mv, rstd, mv_ready, rstd_ready, x1[1 - par], x1_ready)
                if ffn:
                    gelu_tile(t, 1, 1)
                if front:
                    phi_q_main(t, 2, middle)
                if ffn:
                    gelu_tile(t, 1, 2)
                    gelu_tile(t, 1, 3)
                if middle:
                    x1_lo(t)
                if front:
                    phi_k_main(t, 3)
                    phi_q_main(t, 3, middle)

            dve.wait_ge(consts_loaded, 16 * 7)
            dve.wait_ge(qkv_w_loaded, 16 * 4)
            nc.vector.tensor_scalar(w_qkv[:, 0, :], w_qkv_raw[:, 0, :], gam_c, None, ALU.mult).then_inc(qkv_w_ready, 1)
            nc.vector.tensor_scalar(w_qkv[:, 1, :], w_qkv_raw[:, 1, :], gam_c, DH ** -0.5, ALU.mult, ALU.mult)\
                .then_inc(qkv_w_ready, 1)
            nc.vector.tensor_scalar(w_qkv[:, 2, :], w_qkv_raw[:, 2, :], gam_c, None, ALU.mult).then_inc(qkv_w_ready, 1)
            dve.wait_ge(ffn_w_loaded, 16 * 5)
            for n, (raw, a, b) in enumerate(((raw_b, o3, WN), (raw_a, 0, o3))):
                nc.vector.tensor_copy(w_hi[:, a:b], raw[:, 0:b - a]).then_inc(w_hi_ready, 1)
                dve.wait_ge(w_hi_ready, n + 1)
                nc.vector.tensor_tensor(w_lo[:, a:b], raw[:, 0:b - a], w_hi[:, a:b].bitcast(F32), ALU.subtract)\
                    .then_inc(w_ready, 1)
            dve.wait_ge(w_ready, 2)
            nc.vector.tensor_reduce(lo_max[:, :], w_lo[:, :].bitcast(F32), AX.X, ALU.max, apply_absolute_value=True)\
                .then_inc(lo_max_ready, 1)
            dve.wait_ge(lo_max_T, 1)
            nc.vector.tensor_reduce(lo_max1[:, :], ring[0:1, 0, 0:P], AX.X, ALU.max).then_inc(lo_max1_ready, 1)
            steps(dve, step)

        @block.gpsimd
        def _(pool):
            def normed_x(t, par):
                pool.wait_ge(ssc_ready, t + 1)
                nc.gpsimd.tensor_tensor(rn[:, :], ssc[:, :], neg_half, ALU.pow).then_inc(rn_ready, 1)
                pool.wait_ge(rn_ready, t + 1)
                if is_positive(t):
                    pool.wait_ge(ring_full, written(RING, t - 1, "xT"))
                nc.gpsimd.tensor_tensor(xn[:, :, :], x_b[par][:, :, :],
                                        rn[:, :].unsqueeze(2).to_broadcast([P, NT, D]), ALU.mult)\
                    .then_inc(xn_ready, 1)

            def shift8(t, j):
                pool.wait_ge(ring_free[bank_of(RING, f"qkv{j}")], read(RING, t, f"qkv{j}"))
                for rest in (phi_k[:, j, :, MAIN:FEAT], phi_qr[:, j, :, :]):
                    op = nc.gpsimd.tensor_tensor(rest[:, :, PROD8:PROD8 + 8], rest[:, :, 0:8], rest[:, :, 8:16],
                                                 ALU.mult)
                op.then_inc(prod8_ready, 1)

            def weights_rest(t):
                pool.wait_ge(restT_ready, t)
                if is_positive(t - 1):
                    pool.wait_ge(acc_full, 2 * t - 2)
                for g in range(2):
                    src = restT[:, g, :, :].unsqueeze(2).to_broadcast([P, 2, 4, DH])
                    msk = mask.unsqueeze(1).to_broadcast([P, 2, 4, DH])
                    nc.gpsimd.tensor_tensor(w_rest[:, g, :, :, :], src, msk, ALU.mult).then_inc(w_rest_ready, 1)

            def inv_std(n, var_ready, var, rs, rs_ready):
                pool.wait_ge(var_ready, n + 1)
                nc.gpsimd.tensor_tensor(rs[:, :], var[:, :], neg_half[:, :], ALU.pow).then_inc(rs_ready, 1)

            def step(t, par, front, middle, ffn, tail):
                if front:
                    normed_x(t, par)
                if middle:
                    weights_rest(t)
                if front:
                    shift8(t, 0)
                if tail:
                    inv_std(t - 3, zveps_ready, zveps, zrstd, zrstd_ready)
                if front:
                    shift8(t, 1)
                    shift8(t, 2)
                if middle:
                    inv_std(t - 1, veps_ready, veps, rstd, rstd_ready)
                if front:
                    shift8(t, 3)

            nc.gpsimd.memset(phi_qr[:, :, :, ONE:ONE + 1], 1.0)
            nc.gpsimd.memset(w_main[:, :, :, :, :], 0.0)
            nc.gpsimd.memset(v_one[:, :, :, :], 1.0)
            pool.wait_ge(w_ready, 2)
            nc.gpsimd.memset(phi_k[:, :, :, MAIN + ONE:MAIN + ONE + 1], 1.0).then_inc(consts_set, 1)
            pool.wait_ge(consts_loaded, 16 * 7)
            steps(pool, step)


_F = ["L0_ffn_w1", "L0_ffn_w2", "L0_ffn_h1", "L0_ffn_h2", "L0_ffn_w3"]


def kernel(**inputs):
    import numpy as _np
    import concourse.bacc as _bacc
    from concourse import mybir as _mybir
    from concourse.bass_utils import run_bass_kernel_spmd as _run

    a = {k: _np.ascontiguousarray(v) for k, v in inputs.items()}
    data = {
        "x": a["L0_attn_x"], "gamma": a["L0_attn_gamma"].reshape(-1, 1),
        "w_q": a["L0_attn_w_q"], "w_kv": a["L0_attn_w_kv"], "w_out": a["L0_attn_w_out"],
    }
    for name in _F:
        data[name + "_w"] = _np.ascontiguousarray(a[name + "_w"].T)
        data[name + "_s"] = _np.ascontiguousarray(a[name + "_s"].reshape(-1, 128).T)
    row = _np.arange(128)
    used = (row % 32 < DUP) | (row % 32 >= ONE)
    head = (row[:, None] // 32 == _np.arange(4)[None, :]) & used[:, None]
    data["consts"] = _np.concatenate([
        _np.eye(128), _np.repeat(head, DH, axis=1), _np.full((128, 4), -0.5), _np.where(row < DH, 0.5, 1.0)[:, None],
    ], axis=1).astype(_np.float32)

    nc = _bacc.Bacc("TRN2", target_bir_lowering=False, num_devices=1)
    arrays, args = {}, []
    for name, arr in data.items():
        arrays[f"in_{name}"] = arr
        args.append(nc.dram_tensor(f"in_{name}", arr.shape, _mybir.dt.from_np(arr.dtype), kind="ExternalInput").ap())
    args.append(nc.dram_tensor("out_0", data["x"].shape, _mybir.dt.float32, kind="ExternalOutput").ap())
    build(nc, *args)
    r = _run(nc, [arrays], core_ids=[0])
    return r.results[0]["out_0"]
```

```python
from contextlib import ExitStack

import concourse.bass as bass
from concourse import mybir

F32 = mybir.dt.float32
F32R = mybir.dt.float32r
ALU = mybir.AluOpType
ACT = mybir.ActivationFunctionType
AX = mybir.AxisListType

P = 128
H, DH = 8, 16
MAIN, REST = 128, 32
FEAT = MAIN + REST
DUP, ONE, PROD8 = 16, 23, 24
LN_EPS, DEN_EPS, NORM_EPS = 1e-5, 1e-5, 1e-12

FRONT, MIDDLE, FFN, TAIL = range(4)

RING = [(what, stage, n % 2) for n, (what, stage) in enumerate((
    ("state", MIDDLE), ("stateT", MIDDLE), ("xT", FRONT),
    ("phi0", MIDDLE), ("phi2", MIDDLE), ("qkv0", FRONT), ("phi4", MIDDLE), ("phi6", MIDDLE), ("qkv1", FRONT),
    ("phi1", MIDDLE), ("phi3", MIDDLE), ("phi5", MIDDLE), ("phi7", MIDDLE), ("qkv2", FRONT), ("qkv3", FRONT),
    ("out", MIDDLE), ("phi8", FRONT), ("phi9", FRONT)))]
FPS = [(what, stage, n % 4) for n, (what, stage) in enumerate((
    ("a0", FFN), ("b0", FFN), ("a1", FFN), ("b1", FFN), ("a2", FFN), ("b2", FFN), ("a3", FFN), ("b3", FFN),
    ("yT", TAIL), ("two0", FFN), ("two1", FFN), ("two2", FFN), ("two3", FFN),
    ("three0", FFN), ("three1", FFN), ("three2", FFN), ("three3", FFN), ("x1T", MIDDLE), ("y", FFN)))]


def is_positive(count):
    return not isinstance(count, int) or count > 0


def bank_of(table, what):
    return next(b for w, _, b in table if w == what)


def writes_before(table, batches, t, what, bank=None):
    if not isinstance(t, int):
        full = max(stage for _, stage, _ in table)
        per_step = sum(bank in (None, b) for _, _, b in table)
        return per_step * (t - full) + writes_before(table, batches, full, what, bank)
    at = [w for w, _, _ in table].index(what)
    return sum(bank in (None, b) and (step < t or n < at) and 0 <= step - stage < batches
               for step in range(t + 1) for n, (_, stage, b) in enumerate(table))


def build(nc, x, w_q, w_kv, w_out, w1t, w2t, h1t, h2t, w3t, scales, consts, out):
    B, N, D = x.shape
    HID = w1t.shape[1]
    NT = N // P
    KT = HID // P
    assert D == P and H * DH == P and NT == 4 and KT == 4 and B % 2 == 0

    x_d = x.rearrange("b (p j) d -> b p j d", j=NT)
    out_d = out.rearrange("b (p j) d -> b p j d", j=NT)

    with ExitStack() as ctx:
        def sb(name, shape, dt=F32):
            return ctx.enter_context(nc.sbuf_tensor(name, shape, dt))

        def sem(name):
            return ctx.enter_context(nc.semaphore(name))

        ring = ctx.enter_context(nc.psum_tensor("ring", [P, 2, 512], F32))
        acc = ctx.enter_context(nc.psum_tensor("acc", [P, 2, 512], F32))
        fps = ctx.enter_context(nc.psum_tensor("fps", [P, 4, 512], F32))

        w_qkv_raw = sb("w_qkv_raw", [P, 3 * P])
        w_qkv = sb("w_qkv", [P, 3 * P])
        w_qkv_hi = sb("w_qkv_hi", [P, 3 * P], F32R)
        w_qkv_lo = sb("w_qkv_lo", [P, 3 * P], F32R)
        w_o = sb("w_o", [P, P])
        const = sb("const", [P, P + 4 * DH + NT + 1])
        ident = const[:, 0:P]
        mask = const[:, P:P + 4 * DH].rearrange("p (h e) -> p h e", h=4)
        neg_half = const[:, P + 4 * DH:P + 4 * DH + NT]
        half_c = const[:, P + 4 * DH + NT:]
        col = sb("col", [P, 2 + 4 * KT])
        gam_c, s3_c = col[:, 0:1], col[:, 1:2]
        s1_c, s2_c, hs1_c, hs2_c = (col[:, 2 + KT * n:2 + KT * (n + 1)] for n in range(4))
        o1, o2, o3 = 0, HID, 2 * HID
        oh1 = o3 + KT * D
        oh2 = oh1 + KT * HID
        WN = oh2 + KT * HID
        LOADS = (3, 1, 1)
        w_parts = ((0, oh1), (oh1, oh2), (oh2, WN))
        w_hi = sb("w_hi", [P, WN], F32R)
        w_lo = sb("w_lo", [P, WN], F32R)

        x_b = [sb(f"x_b{p}", [P, NT, D]) for p in range(2)]
        sq = sb("sq", [P, NT, D])
        ss = sb("ss", [P, NT])
        ssc = sb("ssc", [P, NT])
        rn = sb("rn", [P, NT])
        xn = sb("xn", [P, NT, D])
        xnT = sb("xnT", [P, N])
        xnT_hi = sb("xnT_hi", [P, N], F32R)
        xnT_lo = sb("xnT_lo", [P, N], F32R)
        v_one = sb("v_one", [P, NT, H, 2 * DH])
        phi_k = sb("phi_k", [P, NT, H, FEAT])
        phi_q = sb("phi_q", [P, NT * H * FEAT])
        phi_qm = phi_q[:, 0:NT * H * MAIN].rearrange("p (j h f) -> p j h f", j=NT, h=H)
        phi_qr = phi_q[:, NT * H * MAIN:].rearrange("p (j h f) -> p j h f", j=NT, h=H)
        st = sb("st", [P, 2, FEAT])
        restT = sb("restT", [P, 2, 2, DH])
        w_main = sb("w_main", [P, 2, 4, 4, DH])
        w_rest = sb("w_rest", [P, 2, 2, 4, DH])
        phiT = sb("phiT", [P, 10, N])
        wide = sb("wide", [P, 4 * N])
        den, rden, att, yT = (wide[:, n * N:(n + 1) * N] for n in range(4))
        x1p = sb("x1p", [P, NT, D])
        stats = sb("stats", [P, NT, 6])
        mv = sb("mv", [P, NT, 2])
        veps = sb("veps", [P, NT])
        rstd = sb("rstd", [P, NT])
        x1 = [sb(f"x1_{p}", [P, NT, D]) for p in range(2)]

        x1T = [sb(f"x1T_{n}", [P, N], F32R) for n in ("hi", "lo")]
        gate_zo = sb("gate_zo", [P, 4 * N])
        gate = gate_zo[:, 0:2 * N].rearrange("p (g n) -> p g n", g=2)
        z, o_b = (gate_zo[:, n * N:(n + 1) * N].rearrange("p (j d) -> p j d", j=NT) for n in (2, 3))
        h32 = sb("h32", [P, 4, N])
        hid = [[sb(f"hid{s}_{n}", [P, KT, N], F32R) for n in ("hi", "lo")] for s in range(2)]
        zstats = sb("zstats", [P, NT, 6])
        zmv = sb("zmv", [P, NT, 2])
        zveps = sb("zveps", [P, NT])
        zrstd = sb("zrstd", [P, NT])
        w_raw = [wide[:, :], h32[:, :, :].rearrange("p k n -> p (k n)"), gate_zo[:, :]]
        table_use = sb("table_use", [P, 1])
        lo_sums = sb("lo_sums", [P, 3])
        lo_max = sb("lo_max", [P, 1])
        lo_max1 = sb("lo_max1", [1, 1])

        consts_loaded, scales_loaded = sem("consts_loaded"), sem("scales_loaded")
        qkv_w_loaded, w_out_loaded = sem("qkv_w_loaded"), sem("w_out_loaded")
        ffn_w_loaded = [sem(f"ffn_w_loaded{n}") for n in range(3)]
        x_loaded = [sem(f"x_loaded{p}") for p in range(2)]
        stored = sem("stored")
        consts_set = sem("consts_set")
        qkv_w_ready = sem("qkv_w_ready")
        w_hi_ready, w_lo_ready = ([sem(f"{n}{part}") for part in range(3)] for n in ("w_hi_ready", "w_lo_ready"))
        lo_sums_ready, lo_max_ready, lo_max_T, lo_max1_ready = (
            sem(n) for n in ("lo_sums_ready", "lo_max_ready", "lo_max_T", "lo_max1_ready"))
        sq_ready, ss_ready, ssc_ready, rn_ready, xn_ready = (
            sem(n) for n in ("sq_ready", "ss_ready", "ssc_ready", "rn_ready", "xn_ready"))
        x_lo_ready = sem("x_lo_ready")
        ring_full = sem("ring_full")
        ring_free = [sem(f"ring_free{b}") for b in range(2)]
        phi_k_ready, prod8_ready = sem("phi_k_ready"), sem("prod8_ready")
        phi_q_ready, phi_q_pool_ready = sem("phi_q_ready"), sem("phi_q_pool_ready")
        restT_ready, w_rest_ready = sem("restT_ready"), sem("w_rest_ready")
        acc_full = sem("acc_full")
        den_ready, rden_ready, att_ready = sem("den_ready"), sem("rden_ready"), sem("att_ready")
        mv_ready, veps_ready, rstd_ready, x1_ready = (
            sem(n) for n in ("mv_ready", "veps_ready", "rstd_ready", "x1_ready"))
        f_full = sem("f_full")
        f_free = [sem(f"f_free{b}") for b in range(4)]
        x1hi_ready = sem("x1hi_ready")
        hi_ready, split_ready = sem("hi_ready"), sem("split_ready")
        zmv_ready, zveps_ready, zrstd_ready, out_ready = (
            sem(n) for n in ("zmv_ready", "zveps_ready", "zrstd_ready", "out_ready"))

        block = ctx.enter_context(nc.Block())

        def peeled(step, t):
            step(t, t % 2, *(0 <= t - stage < B for stage in range(4)))

        def steps_from_2(eng, step):
            peeled(step, 2)
            with eng.Fori(0, B // 2 - 2) as r:
                for half in range(2):
                    step(2 * r + 3 + half, (1 + half) % 2, True, True, True, True)
            for t in range(B - 1, B + 3):
                peeled(step, t)

        def written(table, t, what):
            return writes_before(table, B, t, what) + 1

        def read(table, t, what):
            return writes_before(table, B, t, what, bank_of(table, what)) + 1

        def is_step(t, n):
            return isinstance(t, int) and t == n

        def split_weights(eng, ops, part):
            a, b = w_parts[part]
            eng.wait_ge(w_hi_ready[part], 1)
            ops.tensor_tensor(w_lo[:, a:b], w_raw[part][:, 0:b - a], w_hi[:, a:b].bitcast(F32), ALU.subtract)\
                .then_inc(w_lo_ready[part], 1)

        def products(eng, rest, out):
            base = rest[:, :, 0:DH]
            part, (hs, hn), (es, en) = base.ap[0], base.ap[1], base.ap[2]
            fixed = bass.AP(base.tensor, base.offset, [part, [hs, hn], [0, 8], [es, en]])
            moved = bass.AP(base.tensor, base.offset, [part, [hs, hn], [1, 8], [es, en]])
            return eng.tensor_tensor(out.rearrange("p h (s e) -> p h s e", e=DH), fixed, moved, ALU.mult)

        @block.sync
        def _(sp):
            sp.dma_start(x_b[0][:, :, :], x_d[0]).then_inc(x_loaded[0], 16)
            sp.dma_start(const[:, :], consts).then_inc(consts_loaded, 16)
            sp.dma_start(col[:, :], scales).then_inc(scales_loaded, 16)
            sp.dma_start(w_qkv_raw[:, 0:2 * P], w_kv).then_inc(qkv_w_loaded, 16)
            sp.dma_start(w_qkv_raw[:, 2 * P:], w_q).then_inc(qkv_w_loaded, 16)
            sp.dma_start(w_o[:, :], w_out).then_inc(w_out_loaded, 16)

            def load_ffn_weights():
                for part, weights in enumerate((((o1, w1t), (o2, w2t), (o3, w3t)), ((oh1, h1t),), ((oh2, h2t),))):
                    for o, w in weights:
                        k, n = w.shape[0] // P, w.shape[1]
                        at = o - w_parts[part][0]
                        sp.dma_start(w_raw[part][:, at:at + k * n].rearrange("p (k n) -> p k n", k=k),
                                     w.rearrange("(k p) n -> p k n", p=P)).then_inc(ffn_w_loaded[part], 16)

            def step(t, par, front, middle, ffn, tail):
                if front and not is_step(t, B - 1):
                    if middle:
                        sp.wait_ge(ring_free[bank_of(RING, "out")], read(RING, t, "out"))
                    sp.dma_start(x_b[1 - par][:, :, :],
                                 x_d[bass.ds(t + 1, 1)].rearrange("b p j d -> (b p) j d")
                                 ).then_inc(x_loaded[1 - par], 16)
                if tail:
                    sp.wait_ge(out_ready, t - 2)
                    sp.dma_start(out_d[bass.ds(t - 3, 1)].rearrange("b p j d -> (b p) j d"), o_b[:, :, :])\
                        .then_inc(stored, 16)

            peeled(step, 0)
            load_ffn_weights()
            peeled(step, 1)
            steps_from_2(sp, step)
            sp.wait_ge(stored, 16 * B)

        @block.tensor
        def _(pe):
            def bank_wait(table, free, t, what):
                before = read(table, t, what) - 1
                if is_positive(before):
                    pe.wait_ge(free[bank_of(table, what)], before)

            def transpose_x(t):
                pe.wait_ge(xn_ready, t + 1)
                bank_wait(RING, ring_free, t, "xT")
                for j in range(NT):
                    mm = nc.tensor.transpose(ring[:, bank_of(RING, "xT"), j * P:(j + 1) * P], xn[:, j, :], ident)
                mm.then_inc(ring_full, 1)

            def project_qkv(t, j):
                if j == 0:
                    pe.wait_ge(x_lo_ready, t + 1)
                bank_wait(RING, ring_free, t, f"qkv{j}")
                for n, (x_part, w_part) in enumerate(((xnT_hi, w_qkv_hi), (xnT_hi, w_qkv_lo), (xnT_lo, w_qkv_hi))):
                    mm = nc.tensor.matmul(ring[:, bank_of(RING, f"qkv{j}"), 0:3 * P], x_part[:, j * P:(j + 1) * P],
                                          w_part[:, :], start=(n == 0), stop=(n == 2))
                mm.then_inc(ring_full, 1)

            def state(t):
                bank = bank_of(RING, "state")
                bank_wait(RING, ring_free, t, "state")
                for g in range(2):
                    for j in range(NT):
                        if g == 0:
                            pe.wait_ge(phi_k_ready, NT * (t - 1) + j + 1)
                            pe.wait_ge(prod8_ready, NT * (t - 1) + j + 1)
                        for hh in range(4):
                            mm = nc.tensor.matmul(ring[32 * hh:32 * hh + 32, bank, g * FEAT:(g + 1) * FEAT],
                                                  v_one[:, j, 4 * g + hh, :], phi_k[:, j, 4 * g + hh, :],
                                                  start=(j == 0), stop=(j == NT - 1))
                mm.then_inc(ring_full, 1)

            def transpose_state(t):
                pe.wait_ge(ring_free[bank_of(RING, "state")], read(RING, t, "state"))
                bank_wait(RING, ring_free, t, "stateT")
                for g in range(2):
                    mm = nc.tensor.transpose(ring[:, bank_of(RING, "stateT"), g * P:(g + 1) * P],
                                             st[:, g, 0:MAIN], ident)
                mm.then_inc(ring_full, 1)

            def transpose_phi(t, f):
                what = f"phi{f}"
                bank_wait(RING, ring_free, t, what)
                if f == 8:
                    pe.wait_ge(prod8_ready, NT * (t + 1))
                for j in range(NT):
                    if f == 0 and j < 2:
                        pe.wait_ge(phi_q_ready, 2 * (t - 1) + j + 1)
                    if f == 0 and j >= 2:
                        pe.wait_ge(phi_q_pool_ready, 2 * (t - 1) + j - 1)
                    src = phi_qm[:, j, f, :] if f < H else \
                        phi_qr[:, j, 4 * (f - H):4 * (f - H) + 4, :].rearrange("p h r -> p (h r)")
                    mm = nc.tensor.transpose(ring[:, bank_of(RING, what), j * P:(j + 1) * P], src, ident)
                mm.then_inc(ring_full, 1)

            def apply_main(t, b):
                for f in (b + 4, b + 6):
                    pe.wait_ge(ring_free[bank_of(RING, f"phi{f}")], read(RING, t, f"phi{f}"))
                for nd in range(2):
                    for c in range(4):
                        nc.tensor.matmul(acc[32 * c:32 * c + 32, nd, :],
                                         w_main[:, nd, c, 2 * b:2 * b + 2, :].rearrange("p a e -> p (a e)"),
                                         phiT[:, 2 * c + b, :], start=(b == 0), stop=False)

            def apply_rest(t):
                pe.wait_ge(w_rest_ready, 2 * t)
                for nd in (1, 0):
                    for c in range(4):
                        g, cc = c // 2, c % 2
                        mm = nc.tensor.matmul(acc[32 * c:32 * c + 32, nd, :],
                                              w_rest[:, g, nd, 2 * cc:2 * cc + 2, :].rearrange("p a e -> p (a e)"),
                                              phiT[:, H + g, :], start=False, stop=True)
                    mm.then_inc(acc_full, 1)

            def project_out(t):
                pe.wait_ge(att_ready, t)
                bank_wait(RING, ring_free, t, "out")
                for j in range(NT):
                    mm = nc.tensor.matmul(ring[:, bank_of(RING, "out"), j * P:(j + 1) * P],
                                          att[:, j * P:(j + 1) * P], w_o[:, :], start=True, stop=True)
                mm.then_inc(ring_full, 1)

            def transpose_x1(t, par):
                pe.wait_ge(x1_ready, t)
                bank_wait(FPS, f_free, t, "x1T")
                for j in range(NT):
                    mm = nc.tensor.transpose(fps[:, bank_of(FPS, "x1T"), j * P:(j + 1) * P], x1[par][:, j, :], ident)
                mm.then_inc(f_full, 1)

            def product(bank, o, hi, lo, start, stop, with_lo):
                nc.tensor.matmul(fps[:, bank, :], w_hi[:, o:o + P], hi, start=start, stop=False)
                mm = nc.tensor.matmul(fps[:, bank, :], w_hi[:, o:o + P], lo, start=False, stop=stop and not with_lo)
                if with_lo:
                    mm = nc.tensor.matmul(fps[:, bank, :], w_lo[:, o:o + P], hi, start=False, stop=stop)
                return mm

            def layer1(t, m, with_lo):
                for what, o in ((f"a{m}", o1), (f"b{m}", o2)):
                    bank_wait(FPS, f_free, t, what)
                    if what == "a0":
                        pe.wait_ge(f_free[bank_of(FPS, "x1T")], read(FPS, t - 1, "x1T"))
                    product(bank_of(FPS, what), o + m * P, x1T[0][:, :], x1T[1][:, :], True, True, with_lo)\
                        .then_inc(f_full, 1)

            def hidden(t, what, o, wide, src, before, m, tiles, with_lo):
                for k in tiles:
                    if k == 0:
                        bank_wait(FPS, f_free, t, what)
                    if m == 0:
                        pe.wait_ge(split_ready, 3 * KT * (t - 2) + before + k + 1)
                    mm = product(bank_of(FPS, what), o + k * wide + m * P, hid[src][0][:, k, :],
                                 hid[src][1][:, k, :], k == 0, k == KT - 1, with_lo)
                    if k == KT - 1:
                        mm.then_inc(f_full, 1)

            def layer2(t, m, tiles, with_lo):
                hidden(t, f"two{m}", oh1, HID, 0, 0, m, tiles, with_lo)

            def layer3(t, m, tiles, with_lo):
                hidden(t, f"three{m}", oh2, HID, 1, KT, m, tiles, with_lo)

            def layer4(t, tiles, with_lo):
                hidden(t, "y", o3, D, 0, 2 * KT, 0, tiles, with_lo)

            def transpose_y(t):
                pe.wait_ge(f_free[bank_of(FPS, "y")], read(FPS, t - 1, "y"))
                bank_wait(FPS, f_free, t, "yT")
                for j in range(NT):
                    mm = nc.tensor.transpose(fps[:, bank_of(FPS, "yT"), j * P:(j + 1) * P], yT[:, j * P:(j + 1) * P],
                                             ident)
                mm.then_inc(f_full, 1)

            def steps_with(with_lo):
                def step(t, par, front, middle, ffn, tail):
                    if middle:
                        state(t)
                    if ffn:
                        layer1(t, 0, with_lo)
                    if middle:
                        transpose_state(t)
                    if ffn:
                        layer1(t, 1, with_lo)
                    if front:
                        transpose_x(t)
                    if ffn:
                        layer1(t, 2, with_lo)
                    if middle:
                        transpose_phi(t, 0)
                        transpose_phi(t, 2)
                    if ffn:
                        layer1(t, 3, with_lo)
                    if tail:
                        transpose_y(t)
                    if ffn:
                        layer2(t, 0, (0,), with_lo)
                    if front:
                        project_qkv(t, 0)
                    if ffn:
                        layer2(t, 0, (1,), with_lo)
                    if middle:
                        transpose_phi(t, 4)
                    if ffn:
                        layer2(t, 0, (2,), with_lo)
                    if middle:
                        transpose_phi(t, 6)
                    if ffn:
                        layer2(t, 1, (0,), with_lo)
                    if front:
                        project_qkv(t, 1)
                    if ffn:
                        layer2(t, 1, (1,), with_lo)
                    if middle:
                        transpose_phi(t, 1)
                    if ffn:
                        layer2(t, 0, (3,), with_lo)
                    if middle:
                        transpose_phi(t, 3)
                        apply_main(t, 0)
                        transpose_phi(t, 5)
                    if ffn:
                        layer2(t, 1, (2,), with_lo)
                    if middle:
                        transpose_phi(t, 7)
                    if ffn:
                        layer2(t, 1, (3,), with_lo)
                        layer2(t, 2, (0,), with_lo)
                    if middle:
                        apply_main(t, 1)
                        apply_rest(t)
                    if front:
                        project_qkv(t, 2)
                    if ffn:
                        layer2(t, 2, (1, 2, 3), with_lo)
                    if front:
                        project_qkv(t, 3)
                    if ffn:
                        layer2(t, 3, (0, 1, 2, 3), with_lo)
                        layer3(t, 0, (0, 1, 2), with_lo)
                    if middle:
                        project_out(t)
                    if is_step(t, 1):
                        pe.wait_ge(lo_max_ready, 1)
                        nc.tensor.transpose(fps[0:1, 3, 0:P], lo_max[:, :], ident).then_inc(lo_max_T, 1)
                    if ffn:
                        layer3(t, 1, (0, 1, 2), with_lo)
                        layer3(t, 0, (3,), with_lo)
                        layer3(t, 1, (3,), with_lo)
                        layer3(t, 2, (0, 1, 2, 3), with_lo)
                        layer3(t, 3, (0, 1, 2, 3), with_lo)
                        layer4(t, (0, 1), with_lo)
                    if middle:
                        transpose_x1(t, 1 - par)
                    if ffn:
                        layer4(t, (2,), with_lo)
                    if front:
                        transpose_phi(t, 8)
                    if ffn:
                        layer4(t, (3,), with_lo)
                    if front:
                        transpose_phi(t, 9)

                return step

            pe.wait_ge(consts_loaded, 16)
            pe.wait_ge(qkv_w_ready, 4)
            peeled(steps_with(False), 0)
            pe.wait_ge(w_out_loaded, 16)
            peeled(steps_with(False), 1)
            pe.wait_ge(lo_max1_ready, 1)
            lo_bits = pe.value_load(lo_max1[:, :].bitcast(mybir.dt.int32))
            with pe.If(lo_bits != 0):
                steps_from_2(pe, steps_with(True))
            with pe.Else():
                steps_from_2(pe, steps_with(False))

        @block.scalar
        def _(act):
            def square(t, par):
                act.wait_ge(x_loaded[par], 8 * (t + 2 - par))
                if is_positive(t):
                    act.wait_ge(ss_ready, t)
                nc.scalar.activation(sq[:, :, :], x_b[par][:, :, :], ACT.Square).then_inc(sq_ready, 1)

            def ring_copy(t, what, out, in_, scale=1.0, last=True):
                act.wait_ge(ring_full, written(RING, t, what))
                op = nc.scalar.activation(out, in_, ACT.Copy, scale=scale)
                if last:
                    op.then_inc(ring_free[bank_of(RING, what)], 1)

            def copy_qkv(t, j):
                bank = ring[:, bank_of(RING, f"qkv{j}"), :]
                k, v, q = (bank[:, a * P:(a + 1) * P].rearrange("p (h e) -> p h e", e=DH) for a in range(3))
                if is_positive(t) and j == 0:
                    act.wait_ge(phi_q_ready, 2 * t)
                    act.wait_ge(phi_q_pool_ready, 2 * t)
                    act.wait_ge(prod8_ready, NT * t)
                for src, rest in ((k, phi_k[:, j, :, MAIN:FEAT]), (q, phi_qr[:, j, :, :])):
                    ring_copy(t, f"qkv{j}", rest[:, :, 0:DH], src, last=False)
                    ring_copy(t, f"qkv{j}", rest[:, :, DUP:ONE], src[:, :, 0:ONE - DUP], last=False)
                ring_copy(t, f"qkv{j}", v_one[:, j, :, 0:DH], v)

            def copy_state_T(t):
                src = ring[:, bank_of(RING, "stateT"), 0:2 * P].rearrange("p (c b n e) -> p c b n e", c=4, b=2, n=2)
                for nd in range(2):
                    ring_copy(t, "stateT", w_main[:, nd, :, 0:4:3, :], src[:, :, :, nd, :], half_c, last=(nd == 1))

            def copy_phi_T(t, *tiles):
                for f in tiles:
                    ring_copy(t, f"phi{f}", phiT[:, f, :], ring[:, bank_of(RING, f"phi{f}"), :])

            def x1_hi(t):
                act.wait_ge(f_full, written(FPS, t, "x1T"))
                nc.scalar.activation(x1T[0][:, :], fps[:, bank_of(FPS, "x1T"), :], ACT.Copy).then_inc(x1hi_ready, 1)

            def weights_lo_sum(part):
                act.wait_ge(w_lo_ready[part], 1)
                if part > 0:
                    act.wait_ge(lo_sums_ready, part)
                a, b = w_parts[part]
                nc.scalar.activation(fps[:, :, :].rearrange("p b n -> p (b n)")[:, 0:b - a], w_lo[:, a:b].bitcast(F32),
                                     ACT.Abs, accum_out=lo_sums[:, part:part + 1]).then_inc(lo_sums_ready, 1)

            def load_table(function, source=half_c):
                nc.scalar.activation(table_use[:, :], source, function)

            def silu(t, m):
                act.wait_ge(f_full, written(FPS, t, f"a{m}"))
                if m >= 2:
                    act.wait_ge(f_free[bank_of(FPS, f"b{m - 2}")], read(FPS, t, f"b{m - 2}"))
                nc.scalar.activation(gate[:, m % 2, :], fps[:, bank_of(FPS, f"a{m}"), :], ACT.Silu,
                                     scale=s1_c[:, m:m + 1]).then_inc(f_free[bank_of(FPS, f"a{m}")], 1)

            def gelu(t, layer, m):
                what = f"{('two', 'three')[layer]}{m}"
                n = KT * (layer + 1) + m
                act.wait_ge(f_full, written(FPS, t, what))
                act.wait_ge(split_ready, 3 * KT * (t - 2) + n - 3)
                scale = (hs1_c, hs2_c)[layer][:, m:m + 1]
                bank = bank_of(FPS, what)
                nc.scalar.activation(h32[:, n % 4, :], fps[:, bank, :], ACT.Gelu, scale=scale)
                nc.scalar.activation(hid[1 - layer][0][:, m, :], fps[:, bank, :], ACT.Gelu, scale=scale)\
                    .then_inc(f_free[bank], 1)

            def copy_y(t):
                act.wait_ge(f_full, written(FPS, t, "y"))
                nc.scalar.activation(yT[:, :], fps[:, bank_of(FPS, "y"), :], ACT.Copy, scale=s3_c)\
                    .then_inc(f_free[bank_of(FPS, "y")], 1)

            def step(t, par, front, middle, ffn, tail):
                if ffn:
                    load_table(ACT.Silu)
                if middle:
                    ring_copy(t, "state", st[:, :, :].rearrange("p g f -> p (g f)"),
                              ring[:, bank_of(RING, "state"), 0:2 * FEAT])
                if ffn:
                    silu(t, 0)
                if middle:
                    copy_state_T(t)
                if ffn:
                    silu(t, 1)
                if front:
                    ring_copy(t, "xT", xnT[:, :], ring[:, bank_of(RING, "xT"), :], last=False)
                    ring_copy(t, "xT", xnT_hi[:, :], ring[:, bank_of(RING, "xT"), :])
                if ffn:
                    silu(t, 2)
                if middle:
                    copy_phi_T(t, 0, 2)
                if ffn:
                    silu(t, 3)
                if front:
                    copy_qkv(t, 0)
                if middle:
                    copy_phi_T(t, 4, 6)
                if front:
                    copy_qkv(t, 1)
                if middle:
                    copy_phi_T(t, 1, 3)
                if ffn:
                    load_table(ACT.Gelu)
                if middle:
                    copy_phi_T(t, 5, 7)
                if is_step(t, 1):
                    for part in range(3):
                        weights_lo_sum(part)
                if ffn:
                    gelu(t, 0, 0)
                    gelu(t, 0, 1)
                if front:
                    copy_qkv(t, 2)
                if ffn:
                    gelu(t, 0, 2)
                if front:
                    copy_qkv(t, 3)
                if ffn:
                    gelu(t, 0, 3)
                    gelu(t, 1, 0)
                    gelu(t, 1, 1)
                    gelu(t, 1, 2)
                    gelu(t, 1, 3)
                if middle:
                    x1_hi(t)
                if front:
                    copy_phi_T(t, 8)
                if ffn:
                    copy_y(t)
                if front:
                    copy_phi_T(t, 9)
                if front and not is_step(t, B - 1):
                    square(t + 1, 1 - par)

            act.wait_ge(consts_set, 1)
            load_table(ACT.Square, v_one[:, 0, 0, 0:1])
            square(0, 0)
            peeled(step, 0)
            for part in range(2):
                act.wait_ge(ffn_w_loaded[part], 16 * LOADS[part])
                a, b = w_parts[part]
                nc.scalar.activation(w_hi[:, a:b], w_raw[part][:, 0:b - a], ACT.Copy).then_inc(w_hi_ready[part], 1)
            act.wait_ge(consts_loaded, 16)
            peeled(step, 1)
            act.wait_ge(scales_loaded, 16)
            steps_from_2(act, step)

        @block.vector
        def _(dve):
            def sum_squares(t):
                dve.wait_ge(sq_ready, t + 1)
                nc.vector.tensor_reduce(ss[:, :], sq[:, :, :], AX.X, ALU.add).then_inc(ss_ready, 1)
                dve.wait_ge(ss_ready, t + 1)
                if is_positive(t):
                    dve.wait_ge(rn_ready, t)
                nc.vector.tensor_scalar(ssc[:, :], ss[:, :], NORM_EPS ** 2, 1.0 / D, ALU.max, ALU.mult)\
                    .then_inc(ssc_ready, 1)

            def phi_k_main(t, j):
                dve.wait_ge(ring_free[bank_of(RING, f"qkv{j}")], read(RING, t, f"qkv{j}"))
                products(nc.vector, phi_k[:, j, :, MAIN:FEAT], phi_k[:, j, :, 0:MAIN]).then_inc(phi_k_ready, 1)

            def phi_q_main(t, j, middle):
                dve.wait_ge(ring_free[bank_of(RING, f"qkv{j}")], read(RING, t, f"qkv{j}"))
                if middle and j == 0:
                    dve.wait_ge(ring_full, written(RING, t, "phi7"))
                products(nc.vector, phi_qr[:, j, :, :], phi_qm[:, j, :, :]).then_inc(phi_q_ready, 1)

            def rest_T(t):
                dve.wait_ge(ring_free[bank_of(RING, "state")], read(RING, t, "state"))
                if is_positive(t - 1):
                    dve.wait_ge(w_rest_ready, 2 * t - 2)
                for g in range(2):
                    op = nc.vector.transpose(restT[:, g, :, :].rearrange("p n e -> p (n e)"), st[:, g, MAIN:FEAT])
                op.then_inc(restT_ready, 1)

            def inverse_den(t, half):
                a, b = half * N // 2, (half + 1) * N // 2
                if half == 0:
                    dve.wait_ge(acc_full, 2 * t - 1)
                    nc.vector.tensor_scalar(den, acc[:, 1, :], DEN_EPS, None, ALU.max).then_inc(den_ready, 1)
                    dve.wait_ge(den_ready, t)
                nc.vector.reciprocal(rden[:, a:b], den[:, a:b]).then_inc(rden_ready, 1)

            def normalise(t):
                dve.wait_ge(rden_ready, 2 * t)
                dve.wait_ge(acc_full, 2 * t)
                nc.vector.tensor_tensor(att, acc[:, 0, :], rden, ALU.mult).then_inc(att_ready, 1)

            def norm_scale(n, sm, mv2, rs, s_mv, s_rs, dst, ready):
                dve.wait_ge(s_mv, n + 1)
                dve.wait_ge(s_rs, n + 1)
                for j in range(NT):
                    op = nc.vector.tensor_scalar(dst[:, j, :], sm[:, j, :], mv2[:, j, 0:1], rs[:, j:j + 1],
                                                 ALU.subtract, ALU.mult)
                op.then_inc(ready, 1)

            def sum_x1(t, par):
                bank = bank_of(RING, "out")
                dve.wait_ge(ring_full, written(RING, t, "out"))
                nc.vector.tensor_tensor(x1p[:, :, :].rearrange("p j d -> p (j d)"),
                                        x_b[par][:, :, :].rearrange("p j d -> p (j d)"), ring[:, bank, :],
                                        ALU.add).then_inc(ring_free[bank], 1)
                dve.wait_ge(ring_free[bank], read(RING, t, "out"))
                for j in range(NT):
                    nc.vector.bn_stats(stats[:, j, :], x1p[:, j, :])
                dve.drain()
                for j in range(NT):
                    op = nc.vector.bn_aggr(mv[:, j, :], stats[:, j, :])
                op.then_inc(mv_ready, 1)
                dve.wait_ge(mv_ready, t)
                nc.vector.tensor_scalar(veps[:, :], mv[:, :, 1], LN_EPS, None, ALU.add).then_inc(veps_ready, 1)

            def sum_z(t, par):
                bank = bank_of(FPS, "yT")
                if is_positive(t - 3):
                    dve.wait_ge(out_ready, t - 3)
                dve.wait_ge(f_full, written(FPS, t, "yT"))
                nc.vector.tensor_tensor(z[:, :, :].rearrange("p j d -> p (j d)"),
                                        x1[par][:, :, :].rearrange("p j d -> p (j d)"), fps[:, bank, :],
                                        ALU.add).then_inc(f_free[bank], 1)
                dve.wait_ge(f_free[bank], read(FPS, t, "yT"))
                for j in range(NT):
                    nc.vector.bn_stats(zstats[:, j, :], z[:, j, :])
                dve.drain()
                for j in range(NT):
                    op = nc.vector.bn_aggr(zmv[:, j, :], zstats[:, j, :])
                op.then_inc(zmv_ready, 1)
                dve.wait_ge(zmv_ready, t - 2)
                nc.vector.tensor_scalar(zveps[:, :], zmv[:, :, 1], LN_EPS, None, ALU.add).then_inc(zveps_ready, 1)

            def x1_lo(t):
                bank = bank_of(FPS, "x1T")
                dve.wait_ge(x1hi_ready, t)
                nc.vector.tensor_tensor(x1T[1][:, :], fps[:, bank, :], x1T[0][:, :].bitcast(F32),
                                        ALU.subtract).then_inc(f_free[bank], 1)

            def split(n, dst):
                hi, lo = hid[dst][0][:, n % KT, :], hid[dst][1][:, n % KT, :]
                nc.vector.tensor_tensor(lo, h32[:, n % 4, :], hi.bitcast(F32), ALU.subtract).then_inc(split_ready, 1)

            def gate_mult(t, m):
                a, b = f"a{m}", f"b{m}"
                dve.wait_ge(f_full, written(FPS, t, b))
                dve.wait_ge(f_free[bank_of(FPS, a)], read(FPS, t, a))
                nc.vector.scalar_tensor_tensor(out=h32[:, m, :], in0=fps[:, bank_of(FPS, b), :],
                                               scalar=s2_c[:, m:m + 1], in1=gate[:, m % 2, :], op0=ALU.mult,
                                               op1=ALU.mult).then_inc(f_free[bank_of(FPS, b)], 1)

            def gate_hi(t, m):
                dve.wait_ge(f_free[bank_of(FPS, f"b{m}")], read(FPS, t, f"b{m}"))
                nc.vector.tensor_copy(hid[0][0][:, m, :], h32[:, m, :]).then_inc(hi_ready, 1)

            def gate_lo(t, m):
                dve.wait_ge(hi_ready, KT * (t - 2) + m + 1)
                split(m, 0)

            def gelu_tile(t, layer, m):
                what = f"{('two', 'three')[layer]}{m}"
                dve.wait_ge(f_free[bank_of(FPS, what)], read(FPS, t, what))
                split(KT * (layer + 1) + m, 1 - layer)

            def step(t, par, front, middle, ffn, tail):
                if ffn:
                    gate_mult(t, 0)
                    gate_hi(t, 0)
                    gate_mult(t, 1)
                    gate_lo(t, 0)
                if middle:
                    rest_T(t)
                if is_step(t, 1):
                    split_weights(dve, nc.vector, 1)
                    dve.wait_ge(ffn_w_loaded[2], 16 * LOADS[2])
                    nc.vector.tensor_copy(w_hi[:, oh2:], w_raw[2][:, :]).then_inc(w_hi_ready[2], 1)
                    split_weights(dve, nc.vector, 2)
                if ffn:
                    gate_hi(t, 1)
                    gate_mult(t, 2)
                    gate_lo(t, 1)
                    gate_hi(t, 2)
                    gate_mult(t, 3)
                    gate_lo(t, 2)
                    gate_hi(t, 3)
                    gate_lo(t, 3)
                if tail:
                    sum_z(t, 1 - par)
                if front:
                    phi_k_main(t, 0)
                if tail:
                    if is_positive(t - 3):
                        dve.wait_ge(stored, 16 * (t - 3))
                    norm_scale(t - 3, z, zmv, zrstd, zmv_ready, zrstd_ready, o_b, out_ready)
                if front:
                    phi_k_main(t, 1)
                if is_step(t, 0):
                    phi_k_main(t, 2)
                    phi_k_main(t, 3)
                if front:
                    phi_q_main(t, 0, middle)
                if ffn:
                    gelu_tile(t, 0, 0)
                if front:
                    phi_q_main(t, 1, middle)
                if is_step(t, 1):
                    dve.wait_ge(w_lo_ready[0], 1)
                if middle:
                    inverse_den(t, 0)
                if ffn:
                    gelu_tile(t, 0, 1)
                if middle:
                    inverse_den(t, 1)
                if ffn:
                    gelu_tile(t, 0, 2)
                if middle:
                    normalise(t)
                if front and not is_step(t, 0):
                    phi_k_main(t, 2)
                if ffn:
                    gelu_tile(t, 0, 3)
                if middle:
                    sum_x1(t, 1 - par)
                if is_step(t, 1):
                    largest_lo()
                if front and not is_step(t, 0):
                    phi_k_main(t, 3)
                if ffn:
                    gelu_tile(t, 1, 0)
                    gelu_tile(t, 1, 1)
                if middle:
                    norm_scale(t - 1, x1p, mv, rstd, mv_ready, rstd_ready, x1[1 - par], x1_ready)
                if ffn:
                    gelu_tile(t, 1, 2)
                    gelu_tile(t, 1, 3)
                if middle:
                    x1_lo(t)
                if front and not is_step(t, B - 1):
                    sum_squares(t + 1)

            def largest_lo():
                dve.wait_ge(lo_sums_ready, 3)
                nc.vector.tensor_reduce(lo_max[:, :], lo_sums[:, :], AX.X, ALU.max).then_inc(lo_max_ready, 1)
                dve.wait_ge(lo_max_T, 1)
                nc.vector.tensor_reduce(lo_max1[:, :], fps[0:1, 3, 0:P], AX.X, ALU.max).then_inc(lo_max1_ready, 1)

            dve.wait_ge(scales_loaded, 16)
            dve.wait_ge(qkv_w_loaded, 16 * 2)
            nc.vector.tensor_scalar(w_qkv[:, 0:2 * P], w_qkv_raw[:, 0:2 * P], gam_c, None, ALU.mult)\
                .then_inc(qkv_w_ready, 1)
            nc.vector.tensor_scalar(w_qkv[:, 2 * P:], w_qkv_raw[:, 2 * P:], gam_c, DH ** -0.5, ALU.mult, ALU.mult)\
                .then_inc(qkv_w_ready, 1)
            sum_squares(0)
            dve.wait_ge(qkv_w_ready, 2)
            nc.vector.tensor_copy(w_qkv_hi[:, :], w_qkv[:, :]).then_inc(qkv_w_ready, 1)
            dve.wait_ge(qkv_w_ready, 3)
            nc.vector.tensor_tensor(w_qkv_lo[:, :], w_qkv[:, :], w_qkv_hi[:, :].bitcast(F32), ALU.subtract)\
                .then_inc(qkv_w_ready, 1)
            peeled(step, 0)
            peeled(step, 1)
            steps_from_2(dve, step)

        @block.gpsimd
        def _(pool):
            def normed_x(t, par):
                pool.wait_ge(ssc_ready, t + 1)
                nc.gpsimd.tensor_tensor(rn[:, :], ssc[:, :], neg_half, ALU.pow).then_inc(rn_ready, 1)
                pool.wait_ge(rn_ready, t + 1)
                if is_positive(t):
                    pool.wait_ge(ring_full, written(RING, t - 1, "xT"))
                nc.gpsimd.tensor_tensor(xn[:, :, :], x_b[par][:, :, :],
                                        rn[:, :].unsqueeze(2).to_broadcast([P, NT, D]), ALU.mult)\
                    .then_inc(xn_ready, 1)

            def shift8(t, j):
                pool.wait_ge(ring_free[bank_of(RING, f"qkv{j}")], read(RING, t, f"qkv{j}"))
                for rest in (phi_k[:, j, :, MAIN:FEAT], phi_qr[:, j, :, :]):
                    op = nc.gpsimd.tensor_tensor(rest[:, :, PROD8:PROD8 + 8], rest[:, :, 0:8], rest[:, :, 8:16],
                                                 ALU.mult)
                op.then_inc(prod8_ready, 1)

            def x_lo(t):
                pool.wait_ge(ring_free[bank_of(RING, "xT")], read(RING, t, "xT"))
                nc.gpsimd.tensor_tensor(xnT_lo[:, :], xnT[:, :], xnT_hi[:, :].bitcast(F32), ALU.subtract)\
                    .then_inc(x_lo_ready, 1)

            def weights_rest(t):
                pool.wait_ge(restT_ready, t)
                if is_positive(t - 1):
                    pool.wait_ge(acc_full, 2 * t - 2)
                for g in range(2):
                    src = restT[:, g, :, :].unsqueeze(2).to_broadcast([P, 2, 4, DH])
                    msk = mask.unsqueeze(1).to_broadcast([P, 2, 4, DH])
                    nc.gpsimd.tensor_tensor(w_rest[:, g, :, :, :], src, msk, ALU.mult).then_inc(w_rest_ready, 1)

            def inv_std(n, var_ready, var, rs, rs_ready):
                pool.wait_ge(var_ready, n + 1)
                nc.gpsimd.tensor_tensor(rs[:, :], var[:, :], neg_half[:, :], ALU.pow).then_inc(rs_ready, 1)

            def phi_q_main(t, j, middle):
                pool.wait_ge(ring_free[bank_of(RING, f"qkv{j}")], read(RING, t, f"qkv{j}"))
                if middle and j == 2:
                    pool.wait_ge(ring_full, written(RING, t, "phi7"))
                products(nc.gpsimd, phi_qr[:, j, :, :], phi_qm[:, j, :, :]).then_inc(phi_q_pool_ready, 1)

            def step(t, par, front, middle, ffn, tail):
                if front:
                    x_lo(t)
                if middle:
                    weights_rest(t)
                if front:
                    shift8(t, 0)
                if tail:
                    inv_std(t - 3, zveps_ready, zveps, zrstd, zrstd_ready)
                if front:
                    shift8(t, 1)
                    shift8(t, 2)
                    shift8(t, 3)
                    phi_q_main(t, 2, middle)
                    phi_q_main(t, 3, middle)
                if middle:
                    inv_std(t - 1, veps_ready, veps, rstd, rstd_ready)
                if front and not is_step(t, B - 1):
                    normed_x(t + 1, 1 - par)

            nc.gpsimd.memset(v_one[:, :, :, :], 1.0)
            nc.gpsimd.memset(phi_k[:, :, :, MAIN + ONE:MAIN + ONE + 1], 1.0)
            nc.gpsimd.memset(phi_qr[:, :, :, ONE:ONE + 1], 1.0)
            nc.gpsimd.memset(w_main[:, :, :, :, :], 0.0).then_inc(consts_set, 1)
            pool.wait_ge(consts_loaded, 16)
            normed_x(0, 0)
            peeled(step, 0)
            split_weights(pool, nc.gpsimd, 0)
            peeled(step, 1)
            steps_from_2(pool, step)


def kernel(**inputs):
    import numpy as _np
    import concourse.bacc as _bacc
    from concourse import mybir as _mybir
    from concourse.bass_utils import run_bass_kernel_spmd as _run

    a = {k: _np.ascontiguousarray(v) for k, v in inputs.items()}
    data = {
        "x": a["L0_attn_x"], "w_q": a["L0_attn_w_q"], "w_kv": a["L0_attn_w_kv"], "w_out": a["L0_attn_w_out"],
    }
    for name in ("w1", "w2", "h1", "h2", "w3"):
        data[name] = _np.ascontiguousarray(a[f"L0_ffn_{name}_w"].T)
    columns = [a["L0_attn_gamma"]] + [a[f"L0_ffn_{name}_s"] for name in ("w3", "w1", "w2", "h1", "h2")]
    data["scales"] = _np.concatenate([c.reshape(-1, 128).T for c in columns], axis=1)
    row = _np.arange(128)
    used = (row % 32 < DUP) | (row % 32 >= ONE)
    head = (row[:, None] // 32 == _np.arange(4)[None, :]) & used[:, None]
    data["consts"] = _np.concatenate([
        _np.eye(128), _np.repeat(head, DH, axis=1), _np.full((128, 4), -0.5), _np.where(row < DH, 0.5, 1.0)[:, None],
    ], axis=1).astype(_np.float32)

    nc = _bacc.Bacc("TRN2", target_bir_lowering=False, num_devices=1)
    arrays, args = {}, []
    for name, arr in data.items():
        arrays[f"in_{name}"] = arr
        args.append(nc.dram_tensor(f"in_{name}", arr.shape, _mybir.dt.from_np(arr.dtype), kind="ExternalInput").ap())
    args.append(nc.dram_tensor("out_0", data["x"].shape, _mybir.dt.float32, kind="ExternalOutput").ap())
    build(nc, *args)
    r = _run(nc, [arrays], core_ids=[0])
    return r.results[0]["out_0"]
```
